# Optimizing a Trainium2 kernel written in Bass

```python
import numpy as np
import jax
import jax.numpy as jnp

def _softmax(x, axis=-1):
    return jax.nn.softmax(x, axis=axis)

def _gelu(x):
    return jax.nn.gelu(x, approximate=True)

def _silu(x):
    return jax.nn.silu(x)

def _sigmoid(x):
    return jax.nn.sigmoid(x)

def _layernorm(x, axis=-1, eps=1e-05):
    m = jnp.mean(x, axis=axis, keepdims=True)
    v = jnp.var(x, axis=axis, keepdims=True)
    return (x - m) / jnp.sqrt(v + eps)

def _scatter_add(tgt, idx, src, axis=0):
    return tgt.at[idx].add(src)

def _segment_sum(src, seg, n):
    return jax.ops.segment_sum(src, seg, n)
kernel_name = 'mk_seq_preln_d1_jaxref_r8_60642f'

def setup_inputs(seed: int=0):
    np.random.seed(seed)
    _w = jnp.asarray

    def _L0_attn_setup():
        import jax, jax.numpy as jnp
        import numpy as np
        COSINE_SIM_SCALE = 8.0
        LN_EPS = 1e-05
        HEADS = 8

        def _l2norm(t, eps=1e-12):
            return t * jax.lax.rsqrt(jnp.sum(t * t, axis=-1, keepdims=True) + eps)
        key = jax.random.key(seed)
        k1, k2, k3 = jax.random.split(key, 3)
        b, n, dim = (2, 256, 128)
        inner = 64
        return {'x': jax.random.normal(k1, (b, n, dim), dtype=jnp.float32), 'ln_w': jnp.ones((dim,), dtype=jnp.float32), 'ln_b': jnp.zeros((dim,), dtype=jnp.float32), 'w_qkv': jax.random.normal(k2, (dim, 3 * inner), dtype=jnp.float32) * 0.02, 'w_out': jax.random.normal(k3, (inner, dim), dtype=jnp.float32) * 0.02}
    _L0_attn_in = _L0_attn_setup()

    def _L0_ffn_setup():
        import jax, jax.numpy as jnp
        import numpy as np
        D, H, O, E, TOPK = (128, 512, 128, 8, 2)
        B, S = (4, 128)
        key = jax.random.key(seed)
        ks = jax.random.split(key, 12)
        std = 0.02
        return {'hidden_states': jax.random.normal(ks[0], (B, S, D), dtype=jnp.float32), 'norm_weight': jnp.ones((D,), dtype=jnp.float32), 'router_w': jax.random.normal(ks[1], (E, D), dtype=jnp.float32) * std, 'sw1': jax.random.normal(ks[2], (D, H), dtype=jnp.float32) * (1.0 / np.sqrt(D)), 'sb1': jnp.zeros((H,), dtype=jnp.float32), 'sw2': jax.random.normal(ks[3], (H, O), dtype=jnp.float32) * (1.0 / np.sqrt(H)), 'sb2': jnp.zeros((O,), dtype=jnp.float32), 'ew1': jax.random.normal(ks[4], (E, D, H), dtype=jnp.float32) * (1.0 / np.sqrt(D)), 'eb1': jnp.zeros((E, H), dtype=jnp.float32), 'ew2': jax.random.normal(ks[5], (E, H, O), dtype=jnp.float32) * (1.0 / np.sqrt(H)), 'eb2': jnp.zeros((E, O), dtype=jnp.float32)}
    _L0_ffn_in = _L0_ffn_setup()
    _d = {'L0_attn_x': _L0_attn_in['x'], 'L0_attn_ln_w': _L0_attn_in['ln_w'], 'L0_attn_ln_b': _L0_attn_in['ln_b'], 'L0_attn_w_qkv': _L0_attn_in['w_qkv'], 'L0_attn_w_out': _L0_attn_in['w_out'], 'L0_ffn_norm_weight': _L0_ffn_in['norm_weight'], 'L0_ffn_router_w': _L0_ffn_in['router_w'], 'L0_ffn_sw1': _L0_ffn_in['sw1'], 'L0_ffn_sb1': _L0_ffn_in['sb1'], 'L0_ffn_sw2': _L0_ffn_in['sw2'], 'L0_ffn_sb2': _L0_ffn_in['sb2'], 'L0_ffn_ew1': _L0_ffn_in['ew1'], 'L0_ffn_eb1': _L0_ffn_in['eb1'], 'L0_ffn_ew2': _L0_ffn_in['ew2'], 'L0_ffn_eb2': _L0_ffn_in['eb2']}
    _x0 = _d['L0_attn_x']
    _d['L0_attn_x'] = jax.random.normal(jax.random.fold_in(jax.random.key(seed), 1), (32, 256, 128), dtype=_x0.dtype)
    del _x0
    return _d

def reference(L0_attn_x, L0_attn_ln_w, L0_attn_ln_b, L0_attn_w_qkv, L0_attn_w_out, L0_ffn_norm_weight, L0_ffn_router_w, L0_ffn_sw1, L0_ffn_sb1, L0_ffn_sw2, L0_ffn_sb2, L0_ffn_ew1, L0_ffn_eb1, L0_ffn_ew2, L0_ffn_eb2):

    def _L0_attn_ref(x, ln_w, ln_b, w_qkv, w_out):
        import jax, jax.numpy as jnp
        import numpy as np
        COSINE_SIM_SCALE = 8.0
        LN_EPS = 1e-05
        HEADS = 8

        def _l2norm(t, eps=1e-12):
            return t * jax.lax.rsqrt(jnp.sum(t * t, axis=-1, keepdims=True) + eps)
        b, n, dim = x.shape
        h = HEADS
        mu = jnp.mean(x, axis=-1, keepdims=True)
        var = jnp.mean(jnp.square(x - mu), axis=-1, keepdims=True)
        xn = (x - mu) * jax.lax.rsqrt(var + LN_EPS) * ln_w + ln_b
        qkv = xn @ w_qkv
        q, k, v = jnp.split(qkv, 3, axis=-1)

        def to_heads(t):
            return t.reshape(b, n, h, -1).transpose(0, 2, 1, 3)
        q, k, v = map(to_heads, (q, k, v))
        q = _l2norm(q)
        k = _l2norm(k)
        sim = jnp.einsum('bhid,bhjd->bhij', q, k) * COSINE_SIM_SCALE
        causal_mask = jnp.tril(jnp.ones((n, n), dtype=bool))
        sim = jnp.where(causal_mask, sim, jnp.finfo(sim.dtype).min)
        attn = jax.nn.softmax(sim, axis=-1)
        o = jnp.einsum('bhij,bhjd->bhid', attn, v)
        o = o.transpose(0, 2, 1, 3).reshape(b, n, -1)
        return o @ w_out

    def _L0_ffn_ref(hidden_states, norm_weight, router_w, sw1, sb1, sw2, sb2, ew1, eb1, ew2, eb2):
        import jax, jax.numpy as jnp
        import numpy as np
        D, H, O, E, TOPK = (128, 512, 128, 8, 2)
        B, S = (4, 128)
        b, s, d = hidden_states.shape
        var = jnp.mean(jnp.square(hidden_states), axis=-1, keepdims=True)
        normed = hidden_states * jax.lax.rsqrt(var + 1e-08) * norm_weight
        shared = jnp.maximum(normed @ sw1 + sb1, 0.0) @ sw2 + sb2
        flat = normed.reshape(-1, d)
        T = flat.shape[0]
        probs = jax.nn.sigmoid(flat @ router_w.T)
        scores, idx = jax.lax.top_k(probs, TOPK)
        w = scores / (jnp.sum(scores, axis=-1, keepdims=True) + 1e-06)
        comb = jnp.zeros((T, E), dtype=flat.dtype)
        comb = comb.at[jnp.arange(T)[:, None], idx].add(w)
        h = jnp.maximum(jnp.einsum('td,edh->teh', flat, ew1) + eb1[None, :, :], 0.0)
        eo = jnp.einsum('teh,eho->teo', h, ew2) + eb2[None, :, :]
        routed = jnp.einsum('teo,te->to', eo, comb)
        return shared + routed.reshape(b, s, -1)
    x = L0_attn_x
    x = x + _L0_attn_ref(_layernorm(x, axis=-1), L0_attn_ln_w, L0_attn_ln_b, L0_attn_w_qkv, L0_attn_w_out)
    x = x + _L0_ffn_ref(_layernorm(x, axis=-1), L0_ffn_norm_weight, L0_ffn_router_w, L0_ffn_sw1, L0_ffn_sb1, L0_ffn_sw2, L0_ffn_sb2, L0_ffn_ew1, L0_ffn_eb1, L0_ffn_ew2, L0_ffn_eb2)
    return x

_drawn_inputs = setup_inputs


def setup_inputs(seed=0):
    import zlib

    import numpy as np

    out = dict(_drawn_inputs(seed))
    spreads = {'L0_attn_ln_w': (1.0, 0.2),
     'L0_attn_ln_b': (0.0, 0.277),
     'L0_ffn_norm_weight': (1.0, 0.2),
     'L0_ffn_sb1': (0.0, 0.1),
     'L0_ffn_sb2': (0.0, 0.1),
     'L0_ffn_eb1': (0.0, 0.1),
     'L0_ffn_eb2': (0.0, 0.1)}
    factors = {}
    for name, (base, spread) in spreads.items():
        noise = np.random.default_rng([zlib.crc32(name.encode()), seed]).standard_normal(out[name].shape)
        drawn = base * np.exp(spread * noise) if base else spread * noise
        out[name] = jnp.asarray(drawn.astype(out[name].dtype))
    for name, factor in factors.items():
        out[name] = (out[name] * factor).astype(out[name].dtype)
    return out
```

```python
from contextlib import ExitStack

import concourse.bass as bass
from concourse import mybir


def preln_attention_moe(nc, x_in, ln_w, ln_b, w_qkv, w_out, norm_w, router_w,
                        sw1, sb1, sw2, sb2, ew1, eb1, ew2, eb2, out):
    fp32, fp16, u32 = mybir.dt.float32, mybir.dt.float16, mybir.dt.uint32
    ALU, ACT, AX = mybir.AluOpType, mybir.ActivationFunctionType, mybir.AxisListType

    P = 128
    NSEQ, SEQ, D = x_in.shape
    TPS = SEQ // P
    NT = NSEQ * TPS
    INNER = w_out.shape[0]
    HEADS = 8
    DH = INNER // HEADS
    E, _, H = ew1.shape
    HC = H // P
    NE = E + 1
    TOPK = 2
    SIM = 8.0
    LN_EPS, RMS_EPS, L2_EPS, W_EPS = 1e-5, 1e-8, 1e-12, 1e-6
    QKS = 256.0
    PAIRS = HEADS // 2
    VW = DH + 1
    BT = 4
    NB = NT // BT
    BLK = BT * P

    ctx = ExitStack()
    with ctx:
        def sb(name, shape, dt=fp32):
            return ctx.enter_context(nc.sbuf_tensor(name, shape, dt))

        def pb(name, shape, dt=fp32):
            return ctx.enter_context(nc.psum_tensor(name, shape, dt))

        def sem(name):
            return ctx.enter_context(nc.semaphore(name))

        ident = sb("ident", [P, P])
        ident16 = sb("ident16", [P, P], fp16)
        minus_half = sb("minus_half", [P, 2 * TPS * HEADS])
        expert_no = sb("expert_no", [P, E])
        lnw_sb, lnb_sb, nw_sb = sb("lnw_sb", [P, 1]), sb("lnb_sb", [P, 1]), sb("nw_sb", [P, 1])
        wqkv_sb = sb("wqkv_sb", [P, 3 * INNER])
        wout_sb = sb("wout_sb", [INNER, D])
        rwT_sb = sb("rwT_sb", [P, E])
        w1_sb = sb("w1_sb", [P, NE, H])
        b1_sb = sb("b1_sb", [P, NE, HC])
        w2_sb = sb("w2_sb", [P, NE, HC, D])
        b2_sb = sb("b2_sb", [P, NE, D])
        x_all = sb("x_all", [P, NT, D])
        nT_all = sb("nT_all", [P, NT, P])
        comb = sb("comb", [P, NT, E])
        bn_a, mv_a = sb("bn_a", [P, TPS, 6]), sb("mv_a", [P, TPS, 2])
        var_a, rstd_a = sb("var_a", [P, TPS]), sb("rstd_a", [P, TPS])
        xc = sb("xc", [P, TPS, D])
        xnT = sb("xnT", [P, TPS, P])
        qksq = sb("qksq", [P, TPS, 2 * INNER])
        ss, ss_eps, qk_r = (sb(n, [P, TPS * 2 * HEADS]) for n in ("ss", "ss_eps", "qk_r"))
        qkn = sb("qkn", [P, 2, TPS * HEADS, DH])
        qk16 = sb("qk16", [P, 2, TPS * HEADS, 4, DH], fp16)
        qkT = sb("qkT", [P, 2, TPS, 2, P], fp16)
        vx = [sb(f"vx{u}", [P, TPS, HEADS, VW]) for u in range(2)]
        probs = [sb(f"probs{k}", [P, 2, 3 * P]) for k in range(PAIRS)]
        rsum = sb("rsum", [P, TPS * HEADS])
        o_sb = sb("o_sb", [P, TPS * HEADS, DH])
        oT = sb("oT", [INNER, TPS, P])
        bn_f, mv_f = sb("bn_f", [P, TPS, 6]), sb("mv_f", [P, TPS, 2])
        var_f, rstd_f = sb("var_f", [P, TPS]), sb("rstd_f", [P, TPS])
        z = sb("z", [P, TPS, D])
        nT = [sb(f"nT{u}", [P, TPS, P]) for u in range(2)]
        el = [sb(f"el{u}", [P, TPS, E]) for u in range(2)]
        den, pr = sb("den", [P, TPS, E]), sb("pr", [P, TPS, E])
        top, topi = sb("top", [P, TPS, 8]), sb("topi", [P, TPS, 8], u32)
        topf = sb("topf", [P, TPS, TOPK])
        wsum, rw, wk = sb("wsum", [P, TPS]), sb("rw", [P, TPS]), sb("wk", [P, TPS, TOPK])
        pick = sb("pick", [P, TOPK, TPS, E])
        hT = [sb(f"hT{u}", [P, HC, BLK]) for u in range(2)]
        yb = [sb(f"yb{u}", [P, BT, D]) for u in range(2)]

        bank = [pb(f"bank{k}", [P, 512]) for k in range(8)]
        s_bank = [pb_pair for pb_pair in (bank[0:2], bank[2:4])]

        ctx.enter_context(nc.allow_non_contiguous_dma(reason="small weights, transposed once"))
        block = ctx.enter_context(nc.Block())
        x_loaded = [sem("x_loaded0"), sem("x_loaded1")]
        w_small, w_big = sem("w_small"), sem("w_big")
        consts = sem("consts")
        ident_z = sem("ident_z")
        ident_f = sem("ident_f")
        bn_a_done, mv_a_done, var_a_done, rstd_a_done, xc_done = (sem(n) for n in ("bn_a_done", "mv_a_done", "var_a_done", "rstd_a_done", "xc_done"))
        xT_psum, xnT_done, qkv_psum, sq_done, v_done = (sem(n) for n in ("xT_psum", "xnT_done", "qkv_psum", "sq_done", "v_done"))
        ss_done, eps_done, qkr_done, qkn_done, hi_done, lo_done = (sem(n) for n in ("ss_done", "eps_done", "qkr_done", "qkn_done", "hi_done", "lo_done"))
        qkT_psum, qkT_done = sem("qkT_psum"), sem("qkT_done")
        scores_psum, exp_done, mask_done, pv_psum = (sem(n) for n in ("scores_psum", "exp_done", "mask_done", "pv_psum"))
        rsum_done, o_done, oT_psum, oT_done, proj_psum, x2_done = (sem(n) for n in ("rsum_done", "o_done", "oT_psum", "oT_done", "proj_psum", "x2_done"))
        bn_f_done, mv_f_done, var_f_done, rstd_f_done, z_done = (sem(n) for n in ("bn_f_done", "mv_f_done", "var_f_done", "rstd_f_done", "z_done"))
        zT_psum, nT_done, nT_kept, logits_psum, el_done = (sem(n) for n in ("zT_psum", "nT_done", "nT_kept", "logits_psum", "el_done"))
        route_step, comb_done = sem("route_step"), sem("comb_done")
        up_psum, h_act, h_dve, down_psum, y_done, acc_done, out_sent = (sem(n) for n in ("up_psum", "h_act", "h_dve", "down_psum", "y_done", "acc_done", "out_sent"))
        ROUTE_STEPS = 8

        def wait(eng, semaphore, value):
            if isinstance(value, int) and value <= 0:
                return
            eng.wait_ge(semaphore, value)

        def wait_apart(eng, semaphore, value):
            wait(eng, semaphore, value)
            if not isinstance(value, int):
                eng.nop(nofuse=True)

        STEPS = 5
        ROUNDS = NSEQ + STEPS - 1

        def rounds(eng, body):
            def peeled(i):
                body([i - k if 0 <= i - k < NSEQ else None for k in range(STEPS)], i % 2)
            for i in range(STEPS - 1):
                peeled(i)
            with eng.Fori(STEPS - 1, NSEQ - 1, 2) as r:
                for u in range(2):
                    body([r + (u - k) for k in range(STEPS)], u)
            for i in range(NSEQ, ROUNDS):
                peeled(i)

        def blocks(eng, body):
            for b2 in range(2):
                body(b2, b2)
            with eng.Fori(2, NB - 1, 2) as r:
                for b2 in range(2):
                    body(r + b2, b2)

        def seq_tiles(buf, s):
            return buf[:, bass.ds(s * TPS, TPS), :]

        def seq_tile(buf, s, t):
            return buf[:, bass.ds(s * TPS + t, 1), :]

        @block.sync
        def _(sp):
            def load_x(s, u):
                wait(sp, x_loaded[u], 16 * (s // 2) if isinstance(s, int) else s * 8 - 8 * u)
                sp.dma_start(seq_tiles(x_all, s), x_in[bass.ds(s, 1), :, :].rearrange("s (t p) d -> p (s t) d", p=P)).then_inc(x_loaded[u], 16)
            for s in range(2):
                load_x(s, s)
            small = [(lnw_sb[:, :], ln_w.unsqueeze(1)), (lnb_sb[:, :], ln_b.unsqueeze(1)), (nw_sb[:, :], norm_w.unsqueeze(1)),
                     (wqkv_sb[:, :], w_qkv), (wout_sb[:, :], w_out), (rwT_sb[:, :], router_w.rearrange("e d -> d e"))]
            for dst, src in small:
                sp.dma_start(dst, src).then_inc(w_small, 16)
            with sp.Fori(2, NSEQ - 1, 2) as r:
                for u in range(2):
                    load_x(r + u, u)
            big = [(w1_sb[:, 0:E, :], ew1.rearrange("e d h -> d e h")), (w1_sb[:, E, :], sw1),
                   (b1_sb[:, 0:E, :], eb1.rearrange("e (c p) -> p e c", p=P)), (b1_sb[:, E, :], sb1.rearrange("(c p) -> p c", p=P)),
                   (w2_sb[:, 0:E, :, :], ew2.rearrange("e (c p) o -> p e c o", p=P)), (w2_sb[:, E, :, :], sw2.rearrange("(c p) o -> p c o", p=P)),
                   (b2_sb[:, 0:E, :], eb2.partition_broadcast(P)), (b2_sb[:, E, :], sb2.partition_broadcast(P))]
            for dst, src in big:
                sp.dma_start(dst, src).then_inc(w_big, 16)
            with sp.Fori(0, NB) as b:
                sp.wait_ge(acc_done, (b + 1) * NE)
                sp.dma_start(out.rearrange("s (t p) d -> p (s t) d", p=P)[:, bass.ds(b * BT, BT), :], x_all[:, bass.ds(b * BT, BT), :]).then_inc(out_sent, 16)
            sp.wait_ge(out_sent, 16 * NB)

        SMALL, BIG = 16 * 6, 16 * 8

        @block.tensor
        def _(pe):
            f_bank, k_bank, o_bank, b_bank = bank[4], bank[5], bank[6], bank[7]

            def x_transposes(s):
                pe.wait_ge(xc_done, s + 1)
                wait(pe, qkn_done, s)
                wait(pe, v_done, s)
                for t in range(TPS):
                    mm = nc.tensor.transpose(f_bank[:, t * P:(t + 1) * P], xc[:, t, :], ident[:, :])
                mm.then_inc(xT_psum, 1)

            def qkv(s):
                pe.wait_ge(xnT_done, s + 1)
                for t in range(TPS):
                    mm = nc.tensor.matmul(f_bank[:, t * 3 * INNER:(t + 1) * 3 * INNER], xnT[:, t, :], wqkv_sb[:, :], start=True, stop=True)
                mm.then_inc(qkv_psum, 1)

            def qk_transposes(s):
                pe.wait_ge(hi_done, s + 1)
                pe.wait_ge(lo_done, s + 1)
                wait(pe, qkT_done, s)
                dst = k_bank[:, :].bitcast(fp16)
                for qk in range(2):
                    for t in range(TPS):
                        for g in range(2):
                            n = (qk * TPS + t) * 2 + g
                            src = qk16[:, qk, t * HEADS + 4 * g:t * HEADS + 4 * g + 4, :, :].rearrange("p h c d -> p (h c d)")
                            mm = nc.tensor.transpose(dst[:, n * P:(n + 1) * P], src, ident16[:, :])
                mm.then_inc(qkT_psum, 1)

            def scores(s, k):
                if k == 0:
                    pe.wait_ge(qkT_done, s + 1)
                wait(pe, exp_done, s * PAIRS + k - 1)
                for hh in range(2):
                    g, r = (2 * k + hh) // 4, (2 * k + hh) % 4
                    rows = slice(32 * r, 32 * r + 32)
                    dst = s_bank[k % 2][hh]
                    nc.tensor.matmul(dst[:, 0:3 * P].rearrange("p (b n) -> p b n", b=3)[:, 0:3:2, :], qkT[rows, 1, 0, g, :], qkT[rows, 0, :, g, :], start=True, stop=True)
                    mm = nc.tensor.matmul(dst[:, P:2 * P], qkT[rows, 1, 1, g, :], qkT[rows, 0, 1, g, :], start=True, stop=True)
                mm.then_inc(scores_psum, 1)

            def pv(s, u, k):
                if k == 0:
                    wait(pe, o_done, s)
                    pe.wait_ge(v_done, s + 1)
                pe.wait_ge(mask_done, s * PAIRS + k + 1)
                for hh in range(2):
                    h = 2 * k + hh
                    dst = [o_bank[:, (t * HEADS + h) * VW:(t * HEADS + h + 1) * VW] for t in range(TPS)]
                    p = probs[k]
                    nc.tensor.matmul(dst[0], p[:, hh, 0:P], vx[u][:, 0, h, :], start=True, stop=True)
                    nc.tensor.matmul(dst[1], p[:, hh, 2 * P:3 * P], vx[u][:, 0, h, :], start=True, stop=False)
                    mm = nc.tensor.matmul(dst[1], p[:, hh, P:2 * P], vx[u][:, 1, h, :], start=False, stop=True)
                mm.then_inc(pv_psum, 1)

            def o_transposes(s):
                pe.wait_ge(o_done, s + 1)
                wait_apart(pe, el_done, s)
                for t in range(TPS):
                    mm = nc.tensor.transpose(b_bank[0:INNER, t * P:(t + 1) * P], o_sb[:, t * HEADS:(t + 1) * HEADS, :].rearrange("p h d -> p (h d)"), ident[:, :])
                mm.then_inc(oT_psum, 1)

            def project(s):
                pe.wait_ge(oT_done, s + 1)
                for t in range(TPS):
                    mm = nc.tensor.matmul(b_bank[:, t * D:(t + 1) * D], oT[:, t, :], wout_sb[:, :], start=True, stop=True)
                mm.then_inc(proj_psum, 1)

            def z_transposes(s):
                pe.wait_ge(z_done, s + 1)
                for t in range(TPS):
                    mm = nc.tensor.transpose(b_bank[:, t * P:(t + 1) * P], z[:, t, :], ident[:, :])
                mm.then_inc(zT_psum, 1)

            def route(s, u):
                pe.wait_ge(nT_done, s + 1)
                for t in range(TPS):
                    mm = nc.tensor.matmul(b_bank[:, t * E:(t + 1) * E], nT[u][:, t, :], rwT_sb[:, :], start=True, stop=True)
                mm.then_inc(logits_psum, 1)

            def body(seqs, u):
                _, f, a, b, _ = seqs
                if a is not None:
                    scores(a, 0)
                if f is not None:
                    x_transposes(f)
                if a is not None:
                    scores(a, 1)
                if b is not None:
                    o_transposes(b)
                if a is not None:
                    pv(a, u, 0)
                    scores(a, 2)
                if f is not None:
                    qkv(f)
                if b is not None:
                    project(b)
                if a is not None:
                    pv(a, u, 1)
                    scores(a, 3)
                    pv(a, u, 2)
                if b is not None:
                    z_transposes(b)
                if f is not None:
                    qk_transposes(f)
                if b is not None:
                    route(b, 1 - u)
                if a is not None:
                    pv(a, u, 3)

            pe.wait_ge(w_small, SMALL)
            pe.wait_ge(consts, 2)
            rounds(pe, body)

            pe.wait_ge(w_big, BIG)
            pe.wait_ge(nT_kept, NSEQ)
            pe.wait_ge(el_done, NSEQ)
            pe.wait_ge(comb_done, NSEQ)

            def up(j, b, e):
                wait(pe, h_act, 2 * j)
                for c in range(HC):
                    if c == 2:
                        wait(pe, h_dve, 2 * j)
                    nc.tensor.matmul(bank[c][:, :], w1_sb[:, e, c * P:(c + 1) * P], nT_all[:, bass.ds(b * BT, BT), :],
                                     start=True, stop=True).then_inc(up_psum, 1)

            def down(j, u, e):
                wait(pe, y_done, j - 1)
                pe.wait_ge(h_act, 2 * j + 2)
                pe.wait_ge(h_dve, 2 * j + 2)
                for t in range(BT):
                    for c in range(HC):
                        mm = nc.tensor.matmul(bank[4 + u][:, t * D:(t + 1) * D], hT[u][:, c, t * P:(t + 1) * P], w2_sb[:, e, c, :],
                                              start=(c == 0), stop=(c == HC - 1))
                mm.then_inc(down_psum, 1)

            def block_of_tokens(b, b2):
                for e in range(NE):
                    j = b * NE + e
                    up(j, b, e)
                    down(j, (b2 * NE + e) % 2, e)

            blocks(pe, block_of_tokens)

        @block.scalar
        def _(act):
            f_bank, o_bank, b_bank = bank[4], bank[6], bank[7]

            def softmax_exp(s, k):
                act.wait_ge(scores_psum, s * PAIRS + k + 1)
                wait(act, pv_psum, s * PAIRS + k - 3)
                for hh in range(2):
                    ins = nc.scalar.activation(probs[k][:, hh, :], s_bank[k % 2][hh][:, 0:3 * P], ACT.Exp, scale=SIM / QKS ** 2)
                ins.then_inc(exp_done, 1)

            def body(seqs, u):
                _, f, a, b, _ = seqs
                if a is not None:
                    softmax_exp(a, 0)
                if f is not None:
                    act.wait_ge(xT_psum, f + 1)
                    nc.scalar.activation(xnT[:, :, :].rearrange("p t n -> p (t n)"), f_bank[:, 0:TPS * P], ACT.Identity,
                                         bias=lnb_sb[:, :], scale=lnw_sb[:, :]).then_inc(xnT_done, 1)
                if a is not None:
                    softmax_exp(a, 1)
                if b is not None:
                    act.wait_ge(oT_psum, b + 1)
                    nc.scalar.copy(oT[:, :, :].rearrange("p t n -> p (t n)"), b_bank[0:INNER, 0:TPS * P]).then_inc(oT_done, 1)
                if f is not None:
                    act.wait_ge(qkv_psum, f + 1)
                    qkv = f_bank[:, 0:TPS * 3 * INNER].rearrange("p (t n) -> p t n", t=TPS)
                    nc.scalar.activation(qksq[:, :, :], qkv[:, :, 0:2 * INNER], ACT.Square).then_inc(sq_done, 1)
                    nc.scalar.copy(vx[1 - u][:, :, :, 0:DH], qkv[:, :, 2 * INNER:3 * INNER].rearrange("p t (h d) -> p t h d", d=DH)).then_inc(v_done, 1)
                if a is not None:
                    softmax_exp(a, 2)
                    softmax_exp(a, 3)
                if b is not None:
                    act.wait_ge(zT_psum, b + 1)
                    wait(act, nT_kept, b - 1)
                    nc.scalar.activation(nT[1 - u][:, :, :].rearrange("p t n -> p (t n)"), b_bank[:, 0:TPS * P], ACT.Copy,
                                         scale=nw_sb[:, :]).then_inc(nT_done, 1)
                    act.wait_ge(logits_psum, b + 1)
                    nc.scalar.activation(el[1 - u][:, :, :].rearrange("p t e -> p (t e)"), b_bank[:, 0:TPS * E], ACT.Exp,
                                         scale=-1.0).then_inc(el_done, 1)

            act.wait_ge(w_small, SMALL)
            act.wait_ge(consts, 2)
            rounds(act, body)

            act.wait_ge(w_big, BIG)
            def block_of_tokens(b, b2):
                for e in range(NE):
                    j = b * NE + e
                    u = (b2 * NE + e) % 2
                    wait(act, down_psum, j - 1)
                    for c in range(2):
                        act.wait_ge(up_psum, j * HC + c + 1)
                        nc.scalar.activation(hT[u][:, c, :], bank[c][:, :], ACT.Relu, bias=b1_sb[:, e, c:c + 1]).then_inc(h_act, 1)

            blocks(act, block_of_tokens)

        @block.gpsimd
        def _(pool):
            nc.gpsimd.memset(ident[:, :], 1.0).then_inc(ident_z, 1)
            nc.gpsimd.memset(minus_half[:, :], -0.5)
            nc.gpsimd.iota(expert_no[:, :], [[1, E]], base=0, channel_multiplier=0, allow_small_or_imprecise_dtypes=True)
            for u in range(2):
                nc.gpsimd.memset(vx[u][:, :, :, DH:VW], 1.0)
            pool.wait_ge(ident_z, 1)
            nc.gpsimd.affine_select(out=ident[:, :], in_=ident[:, :], compare_op=ALU.is_equal, fill=0.0, base=0,
                                    pattern=[[-1, P]], channel_multiplier=1).then_inc(consts, 1)
            pool.wait_ge(consts, 1)
            nc.gpsimd.tensor_copy(ident16[:, :], ident[:, :]).then_inc(consts, 1)

            def mask(s, k):
                wait_apart(pool, exp_done, s * PAIRS + k + 1)
                diag = probs[k][:, :, 0:2 * P]
                nc.gpsimd.affine_select(out=diag, in_=diag, compare_op=ALU.is_ge, fill=0.0, base=0,
                                        pattern=[[0, 2], [0, 2], [1, P]], channel_multiplier=-1).then_inc(mask_done, 1)

            def body(seqs, u):
                n, f, a, b, _ = seqs
                if a is not None:
                    mask(a, 0)
                    mask(a, 1)
                if f is not None:
                    pool.wait_ge(eps_done, f + 1)
                    nc.gpsimd.tensor_tensor(qk_r[:, :], ss_eps[:, :], minus_half[:, :], ALU.pow).then_inc(qkr_done, 1)
                if a is not None:
                    mask(a, 2)
                if b is not None:
                    pool.wait_ge(var_f_done, b + 1)
                    nc.gpsimd.tensor_tensor(rstd_f[:, :], var_f[:, :], minus_half[:, 0:TPS], ALU.pow).then_inc(rstd_f_done, 1)
                if f is not None:
                    wait_apart(pool, qkn_done, f + 1)
                    for qk in range(2):
                        dst = qk16[:, 0, :, 0:2, :] if qk == 0 else qk16[:, 1, :, 0:4:2, :]
                        ins = nc.gpsimd.tensor_copy(dst, qkn[:, qk, :, :].unsqueeze(2).broadcast_to((P, TPS * HEADS, 2, DH)))
                    ins.then_inc(hi_done, 1)
                if a is not None:
                    mask(a, 3)
                if n is not None:
                    pool.wait_ge(var_a_done, n + 1)
                    nc.gpsimd.tensor_tensor(rstd_a[:, :], var_a[:, :], minus_half[:, 0:TPS], ALU.pow).then_inc(rstd_a_done, 1)
                if b is not None:
                    wait_apart(pool, nT_done, b + 1)
                    nc.gpsimd.tensor_copy(seq_tiles(nT_all, b), nT[1 - u][:, :, :]).then_inc(nT_kept, 1)

            rounds(pool, body)

        @block.vector
        def _(dve):
            f_bank, k_bank, o_bank, b_bank = bank[4], bank[5], bank[6], bank[7]

            def moments(s, src, bn, mv, bn_done, mv_done):
                for t in range(TPS):
                    ins = nc.vector.bn_stats(bn[:, t, :], seq_tile(src, s, t).rearrange("p a d -> p (a d)"))
                ins.then_inc(bn_done, 1)
                wait_apart(dve, bn_done, s + 1)
                for t in range(TPS):
                    ins = nc.vector.bn_aggr(mv[:, t, :], bn[:, t, :])
                ins.then_inc(mv_done, 1)
                dve.wait_ge(mv_done, s + 1)

            def norm_x(s):
                moments(s, x_all, bn_a, mv_a, bn_a_done, mv_a_done)
                nc.vector.tensor_scalar(var_a[:, :], mv_a[:, :, 1], 1.0 + LN_EPS, LN_EPS * LN_EPS, ALU.mult, ALU.add).then_inc(var_a_done, 1)

            def centre_x(s):
                dve.wait_ge(rstd_a_done, s + 1)
                wait(dve, xT_psum, s)
                for t in range(TPS):
                    ins = nc.vector.tensor_scalar(xc[:, t, :], seq_tile(x_all, s, t).rearrange("p a d -> p (a d)"), mv_a[:, t, 0:1], rstd_a[:, t:t + 1],
                                                  ALU.subtract, ALU.mult)
                ins.then_inc(xc_done, 1)

            def qk_lengths(s):
                dve.wait_ge(sq_done, s + 1)
                nc.vector.reduce_sum(ss[:, :], qksq[:, :, :].rearrange("p t (h d) -> p (t h) d", d=DH), AX.X).then_inc(ss_done, 1)
                dve.wait_ge(ss_done, s + 1)
                nc.vector.tensor_scalar(ss_eps[:, :], ss[:, :], QKS ** -2, L2_EPS * QKS ** -2, ALU.mult, ALU.add).then_inc(eps_done, 1)

            def qk_normalise(s):
                dve.wait_ge(qkr_done, s + 1)
                dve.wait_ge(v_done, s + 1)
                qkv = f_bank[:, 0:TPS * 3 * INNER].rearrange("p (t n) -> p t n", t=TPS)
                r = qk_r[:, :].rearrange("p (t q h) -> p t q h", t=TPS, q=2)
                for qk in range(2):
                    ins = nc.vector.tensor_tensor(qkn[:, qk, :, :].rearrange("p (t h) d -> p t h d", t=TPS),
                                                  qkv[:, :, qk * INNER:(qk + 1) * INNER].rearrange("p t (h d) -> p t h d", d=DH),
                                                  r[:, :, qk, :].unsqueeze(3).broadcast_to((P, TPS, HEADS, DH)), ALU.mult)
                ins.then_inc(qkn_done, 1)

            def qk_low(s):
                dve.wait_ge(hi_done, s + 1)
                dve.wait_ge(qkn_done, s + 1)
                for qk in range(2):
                    dst = qk16[:, 0, :, 2:4, :] if qk == 0 else qk16[:, 1, :, 1:4:2, :]
                    ins = nc.vector.tensor_tensor(dst, qkn[:, qk, :, :].unsqueeze(2).broadcast_to((P, TPS * HEADS, 2, DH)),
                                                  qk16[:, qk, :, 0:1, :].broadcast_to((P, TPS * HEADS, 2, DH)), ALU.subtract)
                ins.then_inc(lo_done, 1)

            def qk_evacuate(s):
                dve.wait_ge(qkT_psum, s + 1)
                nc.vector.tensor_copy(qkT[:, :, :, :, :].rearrange("p q t g n -> p (q t g n)"), k_bank[:, :].bitcast(fp16)).then_inc(qkT_done, 1)

            def normalise_o(s):
                dve.wait_ge(pv_psum, (s + 1) * PAIRS)
                pvo = o_bank[:, 0:TPS * HEADS * VW].rearrange("p (h d) -> p h d", d=VW)
                nc.vector.reciprocal(rsum[:, :], pvo[:, :, DH]).then_inc(rsum_done, 1)
                dve.wait_ge(rsum_done, s + 1)
                nc.vector.tensor_tensor(o_sb[:, :, :], pvo[:, :, 0:DH], rsum[:, :].unsqueeze(2).broadcast_to((P, TPS * HEADS, DH)),
                                        ALU.mult).then_inc(o_done, 1)

            def residual(s):
                dve.wait_ge(proj_psum, s + 1)
                nc.vector.tensor_tensor(seq_tiles(x_all, s), seq_tiles(x_all, s), b_bank[:, 0:TPS * D].rearrange("p (t d) -> p t d", t=TPS),
                                        ALU.add).then_inc(x2_done, 1)
                wait_apart(dve, x2_done, s + 1)
                moments(s, x_all, bn_f, mv_f, bn_f_done, mv_f_done)
                nc.vector.tensor_scalar(var_f[:, :], mv_f[:, :, 1], 1.0 + RMS_EPS, LN_EPS * RMS_EPS, ALU.mult, ALU.add).then_inc(var_f_done, 1)

            def centre_z(s):
                dve.wait_ge(rstd_f_done, s + 1)
                for t in range(TPS):
                    ins = nc.vector.tensor_scalar(z[:, t, :], seq_tile(x_all, s, t).rearrange("p a d -> p (a d)"), mv_f[:, t, 0:1], rstd_f[:, t:t + 1],
                                                  ALU.subtract, ALU.mult)
                ins.then_inc(z_done, 1)

            def routing(s, u):
                def step(n):
                    wait_apart(dve, route_step, s * ROUTE_STEPS + n)
                dve.wait_ge(el_done, s + 1)
                nc.vector.tensor_scalar(den[:, :, :], el[u][:, :, :], 1.0, None, ALU.add).then_inc(route_step, 1)
                step(1)
                nc.vector.reciprocal(pr[:, :, :], den[:, :, :]).then_inc(route_step, 1)
                step(2)
                for t in range(TPS):
                    ins = nc.vector.max(top[:, t, :], pr[:, t, :])
                ins.then_inc(route_step, 1)
                step(3)
                for t in range(TPS):
                    nc.vector.max_index(topi[:, t, :], top[:, t, :], pr[:, t, :])
                nc.vector.scalar_tensor_tensor(wsum[:, :], top[:, :, 0], W_EPS, top[:, :, 1], ALU.add, ALU.add).then_inc(route_step, 1)
                step(4)
                nc.vector.tensor_copy(topf[:, :, :], topi[:, :, 0:TOPK])
                nc.vector.reciprocal(rw[:, :], wsum[:, :]).then_inc(route_step, 1)
                step(5)
                nc.vector.tensor_tensor(wk[:, :, :], top[:, :, 0:TOPK], rw[:, :].unsqueeze(2).broadcast_to((P, TPS, TOPK)), ALU.mult).then_inc(route_step, 1)
                step(6)
                for t in range(TPS):
                    for k in range(TOPK):
                        ins = nc.vector.tensor_scalar(pick[:, k, t, :], expert_no[:, :], topf[:, t, k:k + 1], wk[:, t, k:k + 1], ALU.is_equal, ALU.mult)
                ins.then_inc(route_step, 1)
                step(7)
                nc.vector.tensor_tensor(seq_tiles(comb, s), pick[:, 0, :, :], pick[:, 1, :, :], ALU.add).then_inc(comb_done, 1)
                nc.vector.tensor_copy(topf[:, :, :], wk[:, :, :]).then_inc(route_step, 1)

            def body(seqs, u):
                n, f, a, b, r = seqs
                if a is not None:
                    qk_evacuate(a)
                if b is not None:
                    normalise_o(b)
                if r is not None:
                    routing(r, u)
                if f is not None:
                    qk_lengths(f)
                    qk_normalise(f)
                if b is not None:
                    residual(b)
                if f is not None:
                    qk_low(f)
                if b is not None:
                    centre_z(b)
                if n is not None:
                    wait_apart(dve, x_loaded[u], (n // 2 + 1) * 16 if isinstance(n, int) else n * 8 + (16 - 8 * u))
                    norm_x(n)
                    centre_x(n)

            dve.wait_ge(consts, 2)
            rounds(dve, body)

            dve.wait_ge(w_big, BIG)

            def gate(j, b, u, e):
                dve.wait_ge(down_psum, j + 1)
                nc.vector.tensor_tensor(yb[u][:, :, :], bank[4 + u][:, :].rearrange("p (t d) -> p t d", t=BT),
                                        b2_sb[:, e, :].unsqueeze(1).broadcast_to((P, BT, D)), ALU.add).then_inc(y_done, 1)
                dve.wait_ge(y_done, j + 1)
                wait(dve, acc_done, j)
                if e == E:
                    nc.vector.tensor_tensor(x_all[:, bass.ds(b * BT, BT), :], x_all[:, bass.ds(b * BT, BT), :], yb[u][:, :, :], ALU.add).then_inc(acc_done, 1)
                    return
                for t in range(BT):
                    acc = x_all[:, bass.ds(b * BT + t, 1), :].rearrange("p a d -> p (a d)")
                    g = comb[:, bass.ds(b * BT + t, 1), e:e + 1].rearrange("p a e -> p (a e)")
                    ins = nc.vector.scalar_tensor_tensor(acc, yb[u][:, t, :], g, acc, ALU.mult, ALU.add)
                ins.then_inc(acc_done, 1)

            def block_of_tokens(b, b2):
                for e in range(NE):
                    j = b * NE + e
                    u = (b2 * NE + e) % 2
                    wait(dve, down_psum, j - 1)
                    for c in range(2, HC):
                        dve.wait_ge(up_psum, j * HC + c + 1)
                        nc.vector.tensor_scalar(hT[u][:, c, :], bank[c][:, :], b1_sb[:, e, c:c + 1], 0.0, ALU.add, ALU.max).then_inc(h_dve, 1)
                    gate(j, b, u, e)

            blocks(dve, block_of_tokens)


_INS = ["L0_attn_x", "L0_attn_ln_w", "L0_attn_ln_b", "L0_attn_w_qkv", "L0_attn_w_out", "L0_ffn_norm_weight", "L0_ffn_router_w",
        "L0_ffn_sw1", "L0_ffn_sb1", "L0_ffn_sw2", "L0_ffn_sb2", "L0_ffn_ew1", "L0_ffn_eb1", "L0_ffn_ew2", "L0_ffn_eb2"]


def kernel(**inputs):
    import numpy as _np
    import concourse.bacc as _bacc
    from concourse import mybir as _mybir
    from concourse.bass_utils import run_bass_kernel_spmd as _run

    nc = _bacc.Bacc("TRN2", target_bir_lowering=False, num_devices=1)
    arrays, args = {}, []
    for name in _INS:
        a = _np.ascontiguousarray(inputs[name])
        arrays[f"in_{name}_dram"] = a
        args.append(nc.dram_tensor(f"in_{name}_dram", a.shape, _mybir.dt.from_np(a.dtype), kind="ExternalInput").ap())
    shape = _np.shape(inputs["L0_attn_x"])
    args.append(nc.dram_tensor("out_0_dram", shape, _mybir.dt.float32, kind="ExternalOutput").ap())
    preln_attention_moe(nc, *args)
    r = _run(nc, [arrays], core_ids=[0])
    return r.results[0]["out_0_dram"]
```

```python
from contextlib import ExitStack

import concourse.bass as bass
from concourse import mybir


def preln_attention_moe(nc, x_in, ln_w, ln_b, w_qkv, w_out, norm_w, router_w,
                        sw1, sb1, sw2, sb2, ew1, eb1, ew2, eb2, out):
    fp32, fp16, u32, i32 = mybir.dt.float32, mybir.dt.float16, mybir.dt.uint32, mybir.dt.int32
    ALU, ACT, AX = mybir.AluOpType, mybir.ActivationFunctionType, mybir.AxisListType

    P = 128
    NSEQ, SEQ, D = x_in.shape
    TPS = SEQ // P
    NT = NSEQ * TPS
    INNER = w_out.shape[0]
    HEADS = 8
    DH = INNER // HEADS
    E, _, HC, H1 = ew1.shape
    H = HC * P
    TOPK = 2
    SIM = 8.0
    LN_EPS, RMS_EPS, L2_EPS, W_EPS = 1e-5, 1e-8, 1e-12, 1e-6
    QKS = 256.0
    PAIRS = HEADS // 2
    VW = DH + 1
    BT = 4
    BLK = BT * P
    NB = NT // BT
    TOKENS = NT * P
    REGION = TOKENS + BLK
    SPARE_ROW = E * REGION
    SLOTS = TOPK * TOKENS // BLK + E

    ctx = ExitStack()
    with ctx:
        def sb(name, shape, dt=fp32):
            return ctx.enter_context(nc.sbuf_tensor(name, shape, dt))

        def pb(name, shape, dt=fp32):
            return ctx.enter_context(nc.psum_tensor(name, shape, dt))

        def sem(name):
            return ctx.enter_context(nc.semaphore(name))

        ident = sb("ident", [P, P])
        ident16 = sb("ident16", [P, P], fp16)
        expert_no = sb("expert_no", [P, E])
        lnw_sb, lnb_sb, nw_sb = sb("lnw_sb", [P, 1]), sb("lnb_sb", [P, 1]), sb("nw_sb", [P, 1])
        wqkv_sb = sb("wqkv_sb", [P, 3 * INNER])
        wout_sb = sb("wout_sb", [INNER, D])
        rwT_sb = sb("rwT_sb", [P, E])
        w1_in = [sb(f"w1_in{u}", [P, HC, H1]) for u in range(2)]
        w2_in = [sb(f"w2_in{u}", [P, HC, D]) for u in range(2)]
        b2_in = [sb(f"b2_in{u}", [P, D]) for u in range(2)]
        sw1_sb, sw2_sb, sb2_sb = sb("sw1_sb", [P, HC, H1]), sb("sw2_sb", [P, HC, D]), sb("sb2_sb", [P, D])
        eps_a, eps_f, eps_l2 = sb("eps_a", [P, 1]), sb("eps_f", [P, 1]), sb("eps_l2", [P, 1])
        before, ones16 = sb("before", [P, P], fp16), sb("ones16", [P, P], fp16)
        region_row = sb("region_row", [P, E])
        slot_no = sb("slot_no", [P, SLOTS])
        zeros = sb("zeros", [P, BT, D])
        x_all = sb("x_all", [P, NT, D])
        nT_all = sb("nT_all", [P, NT, P])
        gates = sb("gates", [P, NT, TOPK])
        rows_all = sb("rows_all", [P, NT, TOPK])
        bn_a, mv_a = sb("bn_a", [P, TPS, 6]), sb("mv_a", [P, TPS, 2])
        ln_a, rstd_a = sb("ln_a", [P, TPS]), sb("rstd_a", [P, TPS])
        xc = sb("xc", [P, TPS, D])
        xnT = sb("xnT", [P, TPS, P])
        qksq = sb("qksq", [P, TPS, 2 * INNER])
        ss, ln_ss, qk_r = (sb(n, [P, TPS * 2 * HEADS]) for n in ("ss", "ln_ss", "qk_r"))
        qkn = sb("qkn", [P, 2, TPS * HEADS, DH])
        qk16 = sb("qk16", [P, 2, TPS * HEADS, 4, DH], fp16)
        qkT = sb("qkT", [P, 2, TPS, 2, P], fp16)
        vx = [sb(f"vx{u}", [P, TPS, HEADS, VW]) for u in range(2)]
        probs = [sb(f"probs{k}", [P, 2, 3 * P]) for k in range(PAIRS)]
        rsum = sb("rsum", [P, TPS * HEADS])
        o_sb = sb("o_sb", [P, TPS * HEADS, DH])
        oT = sb("oT", [INNER, TPS, P])
        bn_f, mv_f = sb("bn_f", [P, TPS, 6]), sb("mv_f", [P, TPS, 2])
        ln_f, rstd_f = sb("ln_f", [P, TPS]), sb("rstd_f", [P, TPS])
        z = [sb(f"z{u}", [P, TPS, D]) for u in range(2)]
        nT = [sb(f"nT{u}", [P, TPS, P]) for u in range(2)]
        el = [sb(f"el{u}", [P, TPS, E]) for u in range(2)]
        den, pr = sb("den", [P, TPS, E]), sb("pr", [P, TPS, E])
        top, topi = sb("top", [P, TPS, 8]), sb("topi", [P, TPS, 8], u32)
        topf = sb("topf", [P, TPS, TOPK])
        wsum, rw = sb("wsum", [P, TPS]), sb("rw", [P, TPS])
        chosen = [sb(f"chosen{u}", [P, TPS, TOPK, E]) for u in range(2)]
        picks = [sb(f"picks{u}", [P, TPS, E], fp16) for u in range(2)]
        picked = [sb(f"picked{u}", [P, TPS, E], fp16) for u in range(2)]
        rank, rank_k = sb("rank", [P, TPS, E]), sb("rank_k", [P, TPS, TOPK, E])
        row_f = sb("row_f", [P, TPS, TOPK])
        row_u = [sb(f"row_u{u}", [P, TPS, TOPK], u32) for u in range(2)]
        total16 = sb("total16", [P, E], fp16)
        fill_row = sb("fill_row", [P, E], i32)
        need_i, need_s, need = sb("need_i", [P, E], i32), sb("need_s", [P, E], i32), sb("need", [P, E])
        ends = [sb(f"ends{k}", [P, E]) for k in range(3)]
        skip = sb("skip", [P, E])
        past, past_rows = sb("past", [P, SLOTS, E]), sb("past_rows", [P, SLOTS, E])
        slot_e, slot_row = sb("slot_e", [P, SLOTS]), sb("slot_row", [P, SLOTS])
        slot_row2 = sb("slot_row2", [P, SLOTS])
        slot_ei, slot_ri = (sb(n, [P, SLOTS], i32) for n in ("slot_ei", "slot_ri"))
        rows_out, moved = sb("rows_out", [P, NT * TOPK]), sb("moved", [P, NT * TOPK])
        xs = [sb(f"xs{u}", [P, BT, D]) for u in range(2)]
        xsT = [sb(f"xsT{u}", [P, BLK]) for u in range(2)]
        hT = [sb(f"hT{u}", [P, HC, BLK]) for u in range(2)]
        y = [sb(f"y{u}", [P, BT, D]) for u in range(2)]
        rows_st = [sb(f"rows_st{u}", [P, BT, TOPK], u32) for u in range(2)]
        got = [sb(f"got{u}", [P, BT, TOPK, D]) for u in range(2)]
        sent_rows = nc.dram_tensor("sent_rows", (SPARE_ROW + BLK, D), fp32).ap()
        out_rows = nc.dram_tensor("out_rows", (SLOTS, BLK, D), fp32).ap()

        bank = [pb(f"bank{k}", [P, 512]) for k in range(8)]
        s_bank = [pb_pair for pb_pair in (bank[0:2], bank[2:4])]

        ctx.enter_context(nc.allow_non_contiguous_dma(reason="small weights, transposed once"))
        block = ctx.enter_context(nc.Block())
        def sems(names):
            return (sem(n) for n in names.split())

        x_loaded = [sem("x_loaded0"), sem("x_loaded1")]
        w_small, consts, const_step = sems("w_small consts const_step")
        bn_a_done, mv_a_done, ln_a_done, rstd_a_done, xc_done = sems("bn_a_done mv_a_done ln_a_done rstd_a_done xc_done")
        xT_psum, xnT_done, qkv_psum, sq_done, v_done = sems("xT_psum xnT_done qkv_psum sq_done v_done")
        ss_done, ln_ss_done, qkr_done, qkn_done, hi_done, lo_done = sems("ss_done ln_ss_done qkr_done qkn_done hi_done lo_done")
        qkT_psum, qkT_done, scores_psum, exp_done, mask_done, pv_psum = sems("qkT_psum qkT_done scores_psum exp_done mask_done pv_psum")
        rsum_done, o_done, oT_psum, oT_done, proj_psum, x2_done = sems("rsum_done o_done oT_psum oT_done proj_psum x2_done")
        bn_f_done, mv_f_done, ln_f_done, rstd_f_done, z_done = sems("bn_f_done mv_f_done ln_f_done rstd_f_done z_done")
        zT_psum, nT_done, logits_psum, el_done = sems("zT_psum nT_done logits_psum el_done")
        nT_kept = [sem("nT_kept0"), sem("nT_kept1")]
        route_step, pick_step, picks_done, rank_psum, rank_step, rows_done = sems("route_step pick_step picks_done rank_psum rank_step rows_done")
        rows_sent = [sem("rows_sent0"), sem("rows_sent1")]
        total_done, total_psum, table_step, table_done, filled = sems("total_done total_psum table_step table_done filled")
        xs_in, w1_got, w2_got, b2_got, y_out, got_in = ([sem(f"{n}{u}") for u in range(2)] for n in ("xs_in", "w1_got", "w2_got", "b2_got", "y_out", "got_in"))
        xsT_psum, xsT_done, up_psum, h_done, down_psum, y_done = sems("xsT_psum xsT_done up_psum h_done down_psum y_done")
        rows_staged, acc_step, acc_done, out_sent = sems("rows_staged acc_step acc_done out_sent")
        ROUTE_STEPS, RANK_STEPS = 6, 3

        def wait(eng, semaphore, value):
            if isinstance(value, int) and value <= 0:
                return
            eng.wait_ge(semaphore, value)

        def wait_apart(eng, semaphore, value):
            wait(eng, semaphore, value)
            if not isinstance(value, int):
                eng.nop(nofuse=True)

        LOAD, NORM, FRONT, SOFTMAX, BACK, ROUTE, SEND = range(7)
        STEPS = SEND + 1
        ROUNDS = NSEQ + STEPS - 1

        def rounds(eng, body):
            def one(seq, i):
                body(seq, [(i - k) % 2 for k in range(STEPS)])

            def peeled(i):
                one([i - k if 0 <= i - k < NSEQ else None for k in range(STEPS)], i)
            for i in range(STEPS - 1):
                peeled(i)
            with eng.Fori(STEPS - 1, NSEQ - 1, 2) as r:
                for u in range(2):
                    one([r + (u - k) for k in range(STEPS)], STEPS - 1 + u)
            for i in range(NSEQ, ROUNDS):
                peeled(i)

        def pairs(eng, body, count):
            for j in range(2):
                body(j, j)
            with eng.Fori(2, count - 1, 2) as r:
                for u in range(2):
                    body(r + u, u)

        def in_turn(s, par, per=16):
            return (s // 2 + 1) * per if isinstance(s, int) else s * (per // 2) + (per - par * (per // 2))

        def seq_tiles(buf, s):
            return buf[:, bass.ds(s * TPS, TPS), :]

        def seq_tile(buf, s, t):
            return buf[:, bass.ds(s * TPS + t, 1), :]

        CONSTS = 2
        SMALL = 16 * 9
        UNITS = SLOTS + NB

        @block.sync
        def _(sp):
            small = [(lnw_sb[:, :], ln_w.unsqueeze(1)), (lnb_sb[:, :], ln_b.unsqueeze(1)), (nw_sb[:, :], norm_w.unsqueeze(1)),
                     (wqkv_sb[:, :], w_qkv), (wout_sb[:, :], w_out), (rwT_sb[:, :], router_w),
                     (sw1_sb[:, :, :], sw1[0]), (sw2_sb[:, :, :], sw2[0]), (sb2_sb[:, :], sb2.partition_broadcast(P))]

            def body(seq, par):
                s = seq[LOAD]
                if s is not None:
                    wait(sp, x_loaded[par[LOAD]], in_turn(s, par[LOAD]) - 16)
                    sp.dma_start(seq_tiles(x_all, s), x_in[bass.ds(s, 1), :, :].rearrange("s (t p) d -> p (s t) d", p=P)).then_inc(x_loaded[par[LOAD]], 16)
                if isinstance(s, int) and s == 0:
                    for dst, src in small:
                        sp.dma_start(dst, src).then_inc(w_small, 16)
                s = seq[BACK]
                if s is not None:
                    wait_apart(sp, nT_done, s + 1)
                    sp.dma_start(seq_tiles(nT_all, s), nT[par[BACK]][:, :, :]).then_inc(nT_kept[par[BACK]], 16)

            rounds(sp, body)

            sp.wait_ge(table_done, 1)
            for e in range(E):
                row = sp.value_load(fill_row[0:1, e:e + 1], min_val=e * REGION, max_val=e * REGION + TOKENS)
                sp.dma_start(sent_rows[bass.ds(row, BLK), :].rearrange("(t p) d -> p t d", p=P), zeros[:, :, :]).then_inc(filled, 16)
            sp.dma_start(sent_rows[SPARE_ROW:SPARE_ROW + BLK, :].rearrange("(t p) d -> p t d", p=P), zeros[:, :, :]).then_inc(filled, 16)

            def load_w1(j, u, e):
                sp.dma_start(w1_in[u][:, :, :], ew1[bass.ds(e, 1), :, :, :].rearrange("e p c h -> p (e c) h")).then_inc(w1_got[u], 16)

            def load_w2(j, u, e):
                sp.dma_start(w2_in[u][:, :, :], ew2[bass.ds(e, 1), :, :, :].rearrange("e p c d -> p (e c) d")).then_inc(w2_got[u], 16)

            def load_b2(j, u, e):
                sp.dma_start(b2_in[u][:, :], eb2[bass.ds(e, 1), :].rearrange("e d -> (e d)").partition_broadcast(P)).then_inc(b2_got[u], 16)

            def expert_of(j):
                return sp.value_load(slot_ei[0:1, bass.ds(j, 1)], min_val=0, max_val=E - 1)

            def store(j, u):
                wait_apart(sp, y_done, j + 1)
                sp.dma_start(out_rows[bass.ds(j, 1), :, :].rearrange("j (t p) d -> p (j t) d", p=P), y[u][:, :, :]).then_inc(y_out[u], 16)

            def slot(j, u):
                e = expert_of(j + 2)
                wait_apart(sp, h_done, (j + 1) * HC)
                load_w1(j + 2, u, e)
                wait_apart(sp, down_psum, j + 1)
                load_w2(j + 2, u, e)
                wait_apart(sp, y_done, j + 1)
                load_b2(j + 2, u, e)
                store(j, u)

            for j in range(2):
                e = expert_of(j)
                load_w1(j, j, e)
                load_w2(j, j, e)
                load_b2(j, j, e)
            with sp.Fori(0, SLOTS - 3, 2) as r:
                for u in range(2):
                    slot(r + u, u)
            for j in range(SLOTS - 2, SLOTS):
                store(j, j % 2)

            with sp.Fori(0, NB) as b:
                wait_apart(sp, acc_done, b + 1)
                sp.dma_start(out.rearrange("s (t p) d -> p (s t) d", p=P)[:, bass.ds(b * BT, BT), :], x_all[:, bass.ds(b * BT, BT), :]).then_inc(out_sent, 16)
            sp.wait_ge(out_sent, 16 * NB)

        @block.tensor
        def _(pe):
            f_bank, k_bank, o_bank, b_bank = bank[4], bank[5], bank[6], bank[7]

            def x_transposes(s):
                pe.wait_ge(xc_done, s + 1)
                wait(pe, qkn_done, s)
                wait(pe, v_done, s)
                wait(pe, rank_step, (s - 4) * RANK_STEPS + 1)
                for t in range(TPS):
                    mm = nc.tensor.transpose(f_bank[:, t * P:(t + 1) * P], xc[:, t, :], ident[:, :])
                mm.then_inc(xT_psum, 1)

            def qkv(s):
                pe.wait_ge(xnT_done, s + 1)
                for t in range(TPS):
                    mm = nc.tensor.matmul(f_bank[:, t * 3 * INNER:(t + 1) * 3 * INNER], xnT[:, t, :], wqkv_sb[:, :], start=True, stop=True)
                mm.then_inc(qkv_psum, 1)

            def qk_transposes(s):
                pe.wait_ge(hi_done, s + 1)
                pe.wait_ge(lo_done, s + 1)
                wait(pe, qkT_done, s)
                dst = k_bank[:, :].bitcast(fp16)
                for qk in range(2):
                    for t in range(TPS):
                        for g in range(2):
                            n = (qk * TPS + t) * 2 + g
                            src = qk16[:, qk, t * HEADS + 4 * g:t * HEADS + 4 * g + 4, :, :].rearrange("p h c d -> p (h c d)")
                            mm = nc.tensor.transpose(dst[:, n * P:(n + 1) * P], src, ident16[:, :])
                mm.then_inc(qkT_psum, 1)

            def scores(s, k):
                if k == 0:
                    pe.wait_ge(qkT_done, s + 1)
                wait(pe, exp_done, s * PAIRS + k - 1)
                for hh in range(2):
                    g, r = (2 * k + hh) // 4, (2 * k + hh) % 4
                    rows = slice(32 * r, 32 * r + 32)
                    dst = s_bank[k % 2][hh]
                    nc.tensor.matmul(dst[:, 0:3 * P].rearrange("p (b n) -> p b n", b=3)[:, 0:3:2, :], qkT[rows, 1, 0, g, :], qkT[rows, 0, :, g, :], start=True, stop=True)
                    mm = nc.tensor.matmul(dst[:, P:2 * P], qkT[rows, 1, 1, g, :], qkT[rows, 0, 1, g, :], start=True, stop=True)
                mm.then_inc(scores_psum, 1)

            def pv(s, u, k):
                if k == 0:
                    wait(pe, o_done, s)
                    pe.wait_ge(v_done, s + 1)
                pe.wait_ge(mask_done, s * PAIRS + k + 1)
                for hh in range(2):
                    h = 2 * k + hh
                    dst = [o_bank[:, (t * HEADS + h) * VW:(t * HEADS + h + 1) * VW] for t in range(TPS)]
                    p = probs[k]
                    nc.tensor.matmul(dst[0], p[:, hh, 0:P], vx[u][:, 0, h, :], start=True, stop=True)
                    nc.tensor.matmul(dst[1], p[:, hh, 2 * P:3 * P], vx[u][:, 0, h, :], start=True, stop=False)
                    mm = nc.tensor.matmul(dst[1], p[:, hh, P:2 * P], vx[u][:, 1, h, :], start=False, stop=True)
                mm.then_inc(pv_psum, 1)

            def o_transposes(s):
                pe.wait_ge(o_done, s + 1)
                wait_apart(pe, el_done, s)
                for t in range(TPS):
                    mm = nc.tensor.transpose(b_bank[0:INNER, t * P:(t + 1) * P], o_sb[:, t * HEADS:(t + 1) * HEADS, :].rearrange("p h d -> p (h d)"), ident[:, :])
                mm.then_inc(oT_psum, 1)

            def project(s):
                pe.wait_ge(oT_done, s + 1)
                for t in range(TPS):
                    mm = nc.tensor.matmul(b_bank[:, t * D:(t + 1) * D], oT[:, t, :], wout_sb[:, :], start=True, stop=True)
                mm.then_inc(proj_psum, 1)

            def z_transposes(s, u):
                pe.wait_ge(z_done, s + 1)
                for t in range(TPS):
                    mm = nc.tensor.transpose(b_bank[:, t * P:(t + 1) * P], z[u][:, t, :], ident[:, :])
                mm.then_inc(zT_psum, 1)

            def route(s, u):
                pe.wait_ge(nT_done, s + 1)
                for t in range(TPS):
                    mm = nc.tensor.matmul(b_bank[:, t * E:(t + 1) * E], nT[u][:, t, :], rwT_sb[:, :], start=True, stop=True)
                mm.then_inc(logits_psum, 1)

            def ranks(s, u, front):
                pe.wait_ge(picks_done, s + 1)
                if front is not None:
                    pe.wait_ge(qkn_done, front + 1)
                dst = f_bank[:, 0:TPS * E]
                nc.tensor.matmul(dst, before[:, :], picks[u][:, :, :].rearrange("p t e -> p (t e)"), start=True, stop=False)
                nc.tensor.matmul(dst, ones16[:, :], picked[u][:, :, :].rearrange("p t e -> p (t e)"), start=False, stop=True).then_inc(rank_psum, 1)

            def body(seq, par):
                f, a, b, r = seq[FRONT], seq[SOFTMAX], seq[BACK], seq[ROUTE]
                if a is not None:
                    scores(a, 0)
                if f is not None:
                    x_transposes(f)
                if a is not None:
                    scores(a, 1)
                if b is not None:
                    o_transposes(b)
                if a is not None:
                    pv(a, par[SOFTMAX], 0)
                    scores(a, 2)
                if f is not None:
                    qkv(f)
                if b is not None:
                    project(b)
                if a is not None:
                    pv(a, par[SOFTMAX], 1)
                    scores(a, 3)
                    pv(a, par[SOFTMAX], 2)
                if b is not None:
                    z_transposes(b, par[BACK])
                if f is not None:
                    qk_transposes(f)
                if r is not None:
                    ranks(r, par[ROUTE], f)
                if b is not None:
                    route(b, par[BACK])
                if a is not None:
                    pv(a, par[SOFTMAX], 3)

            pe.wait_ge(w_small, SMALL)
            pe.wait_ge(consts, CONSTS)
            rounds(pe, body)

            pe.wait_ge(total_done, 1)
            nc.tensor.matmul(bank[4][:, 0:E], ones16[:, :], total16[:, :], start=True, stop=True).then_inc(total_psum, 1)

            def row_transposes(j, u):
                pe.wait_ge(xs_in[u], in_turn(j, u))
                wait(pe, xsT_done, j - 1)
                for t in range(BT):
                    mm = nc.tensor.transpose(bank[6 + u][:, t * P:(t + 1) * P], xs[u][:, t, :], ident[:, :])
                mm.then_inc(xsT_psum, 1)

            def up(j, w1, rows):
                for c in range(HC):
                    wait(pe, h_done, (j - 1) * HC + c + 1)
                    nc.tensor.matmul(bank[c][:, :], w1[:, c, 1:H1], rows, start=True, stop=True).then_inc(up_psum, 1)

            def down(j, u, w2):
                pe.wait_ge(h_done, (j + 1) * HC)
                wait(pe, y_done, j - 1)
                for t in range(BT):
                    for c in range(HC):
                        mm = nc.tensor.matmul(bank[4 + u][:, t * D:(t + 1) * D], hT[u][:, c, t * P:(t + 1) * P], w2[:, c, :],
                                              start=(c == 0), stop=(c == HC - 1))
                mm.then_inc(down_psum, 1)

            def expert_down(j, u):
                pe.wait_ge(w2_got[u], in_turn(j, u))
                down(j, u, w2_in[u])

            def slot(j, u, first=False, last=False):
                pe.wait_ge(xsT_done, j + 1)
                pe.wait_ge(w1_got[u], in_turn(j, u))
                up(j, w1_in[u], xsT[u][:, :])
                if not last:
                    row_transposes(j + 1, 1 - u)
                if not first:
                    expert_down(j - 1, 1 - u)

            def shared(b, u, first=False):
                j = b + SLOTS
                up(j, sw1_sb, nT_all[:, bass.ds(b * BT, BT), :])
                if first:
                    expert_down(j - 1, 1 - u)
                else:
                    down(j - 1, 1 - u, sw2_sb)

            pe.wait_ge(table_done, 1)
            row_transposes(0, 0)
            slot(0, 0, first=True)
            slot(1, 1)
            with pe.Fori(2, SLOTS - 3, 2) as r:
                for u in range(2):
                    slot(r + u, u)
            slot(SLOTS - 2, 0)
            slot(SLOTS - 1, 1, last=True)
            for u in range(2):
                pe.wait_ge(nT_kept[u], 16 * (NSEQ // 2))
            shared(0, 0, first=True)
            shared(1, 1)
            with pe.Fori(2, NB - 1, 2) as r:
                for u in range(2):
                    shared(r + u, u)
            down(UNITS - 1, 1, sw2_sb)

        @block.scalar
        def _(act):
            f_bank, o_bank, b_bank = bank[4], bank[6], bank[7]

            def softmax_exp(s, k):
                act.wait_ge(scores_psum, s * PAIRS + k + 1)
                wait(act, pv_psum, s * PAIRS + k - 3)
                for hh in range(2):
                    ins = nc.scalar.activation(probs[k][:, hh, :], s_bank[k % 2][hh][:, 0:3 * P], ACT.Exp, scale=SIM / QKS ** 2)
                ins.then_inc(exp_done, 1)

            def inverse_root(s, dst, tmp, src, eps, scale, step_done, done):
                nc.scalar.activation(tmp, src, ACT.Ln, bias=eps[:, :], scale=scale).then_inc(step_done, 1)
                act.wait_ge(step_done, s + 1)
                nc.scalar.activation(dst, tmp, ACT.Exp, scale=-0.5).then_inc(done, 1)

            def body(seq, par):
                n, f, a, b = seq[NORM], seq[FRONT], seq[SOFTMAX], seq[BACK]
                if a is not None:
                    softmax_exp(a, 0)
                if f is not None:
                    act.wait_ge(xT_psum, f + 1)
                    nc.scalar.activation(xnT[:, :, :].rearrange("p t n -> p (t n)"), f_bank[:, 0:TPS * P], ACT.Identity,
                                         bias=lnb_sb[:, :], scale=lnw_sb[:, :]).then_inc(xnT_done, 1)
                if a is not None:
                    softmax_exp(a, 1)
                if b is not None:
                    act.wait_ge(oT_psum, b + 1)
                    nc.scalar.copy(oT[:, :, :].rearrange("p t n -> p (t n)"), b_bank[0:INNER, 0:TPS * P]).then_inc(oT_done, 1)
                if f is not None:
                    act.wait_ge(qkv_psum, f + 1)
                    qkv = f_bank[:, 0:TPS * 3 * INNER].rearrange("p (t n) -> p t n", t=TPS)
                    nc.scalar.activation(qksq[:, :, :], qkv[:, :, 0:2 * INNER], ACT.Square).then_inc(sq_done, 1)
                    nc.scalar.copy(vx[par[FRONT]][:, :, :, 0:DH], qkv[:, :, 2 * INNER:3 * INNER].rearrange("p t (h d) -> p t h d", d=DH)).then_inc(v_done, 1)
                if a is not None:
                    softmax_exp(a, 2)
                if f is not None:
                    act.wait_ge(ss_done, f + 1)
                    inverse_root(f, qk_r[:, :], ln_ss[:, :], ss[:, :], eps_l2, QKS ** -2, ln_ss_done, qkr_done)
                if a is not None:
                    softmax_exp(a, 3)
                if b is not None:
                    act.wait_ge(mv_f_done, b + 1)
                    inverse_root(b, rstd_f[:, :], ln_f[:, :], mv_f[:, :, 1], eps_f, 1.0 + RMS_EPS, ln_f_done, rstd_f_done)
                if n is not None:
                    act.wait_ge(mv_a_done, n + 1)
                    inverse_root(n, rstd_a[:, :], ln_a[:, :], mv_a[:, :, 1], eps_a, 1.0 + LN_EPS, ln_a_done, rstd_a_done)
                if b is not None:
                    act.wait_ge(zT_psum, b + 1)
                    wait(act, nT_kept[par[BACK]], in_turn(b, par[BACK]) - 16)
                    nc.scalar.activation(nT[par[BACK]][:, :, :].rearrange("p t n -> p (t n)"), b_bank[:, 0:TPS * P], ACT.Copy,
                                         scale=nw_sb[:, :]).then_inc(nT_done, 1)
                    act.wait_ge(logits_psum, b + 1)
                    nc.scalar.activation(el[par[BACK]][:, :, :].rearrange("p t e -> p (t e)"), b_bank[:, 0:TPS * E], ACT.Exp,
                                         scale=-1.0).then_inc(el_done, 1)

            act.wait_ge(w_small, SMALL)
            act.wait_ge(consts, CONSTS)
            rounds(act, body)

            def rows_scaled(j, u):
                act.wait_ge(xsT_psum, j + 1)
                nc.scalar.activation(xsT[u][:, :], bank[6 + u][:, :], ACT.Copy, scale=nw_sb[:, :]).then_inc(xsT_done, 1)

            def hidden(j, u, w1):
                wait(act, down_psum, j - 1)
                for c in range(HC):
                    act.wait_ge(up_psum, j * HC + c + 1)
                    nc.scalar.activation(hT[u][:, c, :], bank[c][:, :], ACT.Relu, bias=w1[:, c, 0:1]).then_inc(h_done, 1)

            def slot(j, u, last=False):
                hidden(j, u, w1_in[u])
                if not last:
                    rows_scaled(j + 1, 1 - u)

            rows_scaled(0, 0)
            slot(0, 0)
            slot(1, 1)
            with act.Fori(2, SLOTS - 3, 2) as r:
                for u in range(2):
                    slot(r + u, u)
            slot(SLOTS - 2, 0)
            slot(SLOTS - 1, 1, last=True)
            with act.Fori(0, NB - 1, 2) as r:
                for u in range(2):
                    hidden(r + (u + SLOTS), u, sw1_sb)

        @block.gpsimd
        def _(pool):
            nc.gpsimd.memset(ident[:, :], 1.0)
            nc.gpsimd.memset(before[:, :], 1.0)
            nc.gpsimd.memset(ones16[:, :], 1.0)
            nc.gpsimd.memset(zeros[:, :, :], 0.0)
            nc.gpsimd.memset(eps_a[:, :], LN_EPS * LN_EPS)
            nc.gpsimd.memset(eps_f[:, :], LN_EPS * RMS_EPS)
            nc.gpsimd.memset(eps_l2[:, :], L2_EPS * QKS ** -2)
            for u in range(2):
                nc.gpsimd.memset(picks[u][:, :, :], 0.0)
                nc.gpsimd.memset(picked[u][:, :, :], 0.0)
                nc.gpsimd.memset(vx[u][:, :, :, DH:VW], 1.0)
            nc.gpsimd.iota(expert_no[:, :], [[1, E]], base=0, channel_multiplier=0, allow_small_or_imprecise_dtypes=True)
            nc.gpsimd.iota(region_row[:, :], [[REGION, E]], base=0, channel_multiplier=0, allow_small_or_imprecise_dtypes=True)
            nc.gpsimd.iota(slot_no[:, :], [[1, SLOTS]], base=0, channel_multiplier=0, allow_small_or_imprecise_dtypes=True).then_inc(const_step, 1)
            pool.wait_ge(const_step, 1)
            nc.gpsimd.affine_select(out=ident[:, :], in_=ident[:, :], compare_op=ALU.is_equal, fill=0.0, base=0,
                                    pattern=[[-1, P]], channel_multiplier=1).then_inc(consts, 1)
            nc.gpsimd.affine_select(out=before[:, :], in_=before[:, :], compare_op=ALU.is_gt, fill=0.0, base=0,
                                    pattern=[[1, P]], channel_multiplier=-1)
            pool.wait_ge(consts, 1)
            nc.gpsimd.tensor_copy(ident16[:, :], ident[:, :]).then_inc(consts, 1)

            def mask(s, k):
                wait_apart(pool, exp_done, s * PAIRS + k + 1)
                diag = probs[k][:, :, 0:2 * P]
                nc.gpsimd.affine_select(out=diag, in_=diag, compare_op=ALU.is_ge, fill=0.0, base=0,
                                        pattern=[[0, 2], [0, 2], [1, P]], channel_multiplier=-1).then_inc(mask_done, 1)

            def send(s, u, t):
                for k in range(TOPK):
                    nc.gpsimd.indirect_dma_start(out=sent_rows, out_offset=bass.IndirectOffsetOnAxis(ap=row_u[u][:, t, k:k + 1], axis=0),
                                                 in_=z[u][:, t, :], in_offset=None).then_inc(rows_sent[u], 16)

            def body(seq, par):
                f, a, d = seq[FRONT], seq[SOFTMAX], seq[SEND]
                if a is not None:
                    mask(a, 0)
                if d is not None:
                    wait_apart(pool, rows_done, d + 1)
                    send(d, par[SEND], 0)
                if a is not None:
                    mask(a, 1)
                if d is not None:
                    send(d, par[SEND], 1)
                if a is not None:
                    mask(a, 2)
                if f is not None:
                    wait_apart(pool, qkn_done, f + 1)
                    for qk in range(2):
                        dst = qk16[:, 0, :, 0:2, :] if qk == 0 else qk16[:, 1, :, 0:4:2, :]
                        ins = nc.gpsimd.tensor_copy(dst, qkn[:, qk, :, :].unsqueeze(2).broadcast_to((P, TPS * HEADS, 2, DH)))
                    ins.then_inc(hi_done, 1)
                if a is not None:
                    mask(a, 3)

            rounds(pool, body)

            def load_rows(j, u):
                row = pool.value_load(slot_ri[0:1, bass.ds(j, 1)], min_val=0, max_val=SPARE_ROW)
                pool.dma_start(xs[u][:, :, :], sent_rows[bass.ds(row, BLK), :].rearrange("(t p) d -> p t d", p=P)).then_inc(xs_in[u], 16)

            pool.wait_ge(table_done, 1)
            for u in range(2):
                pool.wait_ge(rows_sent[u], 16 * TPS * TOPK * (NSEQ // 2))
            pool.wait_ge(filled, 16 * (E + 1))
            for j in range(2):
                load_rows(j, j)
            with pool.Fori(2, SLOTS - 1, 2) as r:
                for u in range(2):
                    wait_apart(pool, xsT_psum, r + (u - 1))
                    load_rows(r + u, u)

            def gather(b, u):
                wait_apart(pool, acc_done, b - 1)
                wait_apart(pool, rows_staged, b + 1)
                for t in range(BT):
                    for k in range(TOPK):
                        nc.gpsimd.indirect_dma_start(out=got[u][:, t, k, :], out_offset=None, in_=out_rows.rearrange("j n d -> (j n) d"),
                                                     in_offset=bass.IndirectOffsetOnAxis(ap=rows_st[u][:, t, k:k + 1], axis=0)).then_inc(got_in[u], 16)

            for u in range(2):
                pool.wait_ge(y_out[u], 16 * (SLOTS // 2))
            pairs(pool, gather, NB)

        @block.vector
        def _(dve):
            f_bank, k_bank, o_bank, b_bank = bank[4], bank[5], bank[6], bank[7]

            def moments(s, src, bn, mv, bn_done, mv_done):
                for t in range(TPS):
                    ins = nc.vector.bn_stats(bn[:, t, :], seq_tile(src, s, t).rearrange("p a d -> p (a d)"))
                ins.then_inc(bn_done, 1)
                wait_apart(dve, bn_done, s + 1)
                for t in range(TPS):
                    ins = nc.vector.bn_aggr(mv[:, t, :], bn[:, t, :])
                ins.then_inc(mv_done, 1)

            def centre(s, dst, mv, rstd, done):
                for t in range(TPS):
                    ins = nc.vector.tensor_scalar(dst[:, t, :], seq_tile(x_all, s, t).rearrange("p a d -> p (a d)"), mv[:, t, 0:1], rstd[:, t:t + 1],
                                                  ALU.subtract, ALU.mult)
                ins.then_inc(done, 1)

            def qk_lengths(s):
                dve.wait_ge(sq_done, s + 1)
                nc.vector.reduce_sum(ss[:, :], qksq[:, :, :].rearrange("p t (h d) -> p (t h) d", d=DH), AX.X).then_inc(ss_done, 1)

            def qk_normalise(s):
                dve.wait_ge(v_done, s + 1)
                dve.wait_ge(qkr_done, s + 1)
                qkv = f_bank[:, 0:TPS * 3 * INNER].rearrange("p (t n) -> p t n", t=TPS)
                r = qk_r[:, :].rearrange("p (t q h) -> p t q h", t=TPS, q=2)
                for qk in range(2):
                    ins = nc.vector.tensor_tensor(qkn[:, qk, :, :].rearrange("p (t h) d -> p t h d", t=TPS),
                                                  qkv[:, :, qk * INNER:(qk + 1) * INNER].rearrange("p t (h d) -> p t h d", d=DH),
                                                  r[:, :, qk, :].unsqueeze(3).broadcast_to((P, TPS, HEADS, DH)), ALU.mult)
                ins.then_inc(qkn_done, 1)

            def qk_low(s):
                dve.wait_ge(hi_done, s + 1)
                for qk in range(2):
                    dst = qk16[:, 0, :, 2:4, :] if qk == 0 else qk16[:, 1, :, 1:4:2, :]
                    ins = nc.vector.tensor_tensor(dst, qkn[:, qk, :, :].unsqueeze(2).broadcast_to((P, TPS * HEADS, 2, DH)),
                                                  qk16[:, qk, :, 0:1, :].broadcast_to((P, TPS * HEADS, 2, DH)), ALU.subtract)
                ins.then_inc(lo_done, 1)

            def qk_evacuate(s):
                dve.wait_ge(qkT_psum, s + 1)
                nc.vector.tensor_copy(qkT[:, :, :, :, :].rearrange("p q t g n -> p (q t g n)"), k_bank[:, :].bitcast(fp16)).then_inc(qkT_done, 1)

            def normalise_o(s):
                dve.wait_ge(pv_psum, (s + 1) * PAIRS)
                pvo = o_bank[:, 0:TPS * HEADS * VW].rearrange("p (h d) -> p h d", d=VW)
                nc.vector.reciprocal(rsum[:, :], pvo[:, :, DH]).then_inc(rsum_done, 1)
                dve.wait_ge(rsum_done, s + 1)
                nc.vector.tensor_tensor(o_sb[:, :, :], pvo[:, :, 0:DH], rsum[:, :].unsqueeze(2).broadcast_to((P, TPS * HEADS, DH)),
                                        ALU.mult).then_inc(o_done, 1)

            def residual(s):
                dve.wait_ge(proj_psum, s + 1)
                nc.vector.tensor_tensor(seq_tiles(x_all, s), seq_tiles(x_all, s), b_bank[:, 0:TPS * D].rearrange("p (t d) -> p t d", t=TPS),
                                        ALU.add).then_inc(x2_done, 1)
                wait_apart(dve, x2_done, s + 1)
                moments(s, x_all, bn_f, mv_f, bn_f_done, mv_f_done)

            def choose(s, u):
                def step(n):
                    wait_apart(dve, route_step, s * ROUTE_STEPS + n)
                dve.wait_ge(el_done, s + 1)
                nc.vector.tensor_scalar(den[:, :, :], el[u][:, :, :], 1.0, None, ALU.add).then_inc(route_step, 1)
                step(1)
                nc.vector.reciprocal(pr[:, :, :], den[:, :, :]).then_inc(route_step, 1)
                step(2)
                for t in range(TPS):
                    ins = nc.vector.max(top[:, t, :], pr[:, t, :])
                ins.then_inc(route_step, 1)
                step(3)
                for t in range(TPS):
                    nc.vector.max_index(topi[:, t, :], top[:, t, :], pr[:, t, :])
                nc.vector.scalar_tensor_tensor(wsum[:, :], top[:, :, 0], W_EPS, top[:, :, 1], ALU.add, ALU.add).then_inc(route_step, 1)
                step(4)
                nc.vector.tensor_copy(topf[:, :, :], topi[:, :, 0:TOPK])
                nc.vector.reciprocal(rw[:, :], wsum[:, :]).then_inc(route_step, 1)
                step(5)
                nc.vector.tensor_tensor(chosen[u][:, :, :, :].rearrange("p t k e -> p (t k) e"), expert_no[:, :].unsqueeze(1).broadcast_to((P, TPS * TOPK, E)),
                                        topf[:, :, :].rearrange("p t k -> p (t k)").unsqueeze(2).broadcast_to((P, TPS * TOPK, E)), ALU.is_equal)
                nc.vector.tensor_tensor(seq_tiles(gates, s), top[:, :, 0:TOPK], rw[:, :].unsqueeze(2).broadcast_to((P, TPS, TOPK)), ALU.mult)
                nc.vector.tensor_tensor(picked[u][:, 0, :], picked[1 - u][:, 1, :], picks[1 - u][:, 1, :], ALU.add).then_inc(route_step, 1)
                step(6)
                nc.vector.tensor_tensor(picks[u][:, :, :], chosen[u][:, :, 0, :], chosen[u][:, :, 1, :], ALU.add)
                nc.vector.tensor_tensor(picked[u][:, 1, :], picked[u][:, 0, :], chosen[u][:, 0, 0, :], ALU.add).then_inc(pick_step, 1)
                wait_apart(dve, pick_step, s + 1)
                nc.vector.tensor_tensor(picked[u][:, 1, :], picked[u][:, 1, :], chosen[u][:, 0, 1, :], ALU.add).then_inc(picks_done, 1)

            def number(s, u):
                dve.wait_ge(rank_psum, s + 1)
                nc.vector.tensor_tensor(rank[:, :, :], f_bank[:, 0:TPS * E].rearrange("p (t e) -> p t e", t=TPS),
                                        region_row[:, :].unsqueeze(1).broadcast_to((P, TPS, E)), ALU.add).then_inc(rank_step, 1)
                dve.wait_ge(rank_step, s * RANK_STEPS + 1)
                nc.vector.tensor_tensor(rank_k[:, :, :, :], chosen[u][:, :, :, :], rank[:, :, :].unsqueeze(2).broadcast_to((P, TPS, TOPK, E)),
                                        ALU.mult).then_inc(rank_step, 1)
                dve.wait_ge(rank_step, s * RANK_STEPS + 2)
                nc.vector.reduce_sum(row_f[:, :, :], rank_k[:, :, :, :], AX.X).then_inc(rank_step, 1)
                dve.wait_ge(rank_step, s * RANK_STEPS + 3)
                nc.vector.tensor_copy(row_u[u][:, :, :], row_f[:, :, :]).then_inc(rows_done, 1)
                nc.vector.tensor_copy(seq_tiles(rows_all, s), row_f[:, :, :])

            def body(seq, par):
                n, f, a, b, r = (seq[k] for k in (NORM, FRONT, SOFTMAX, BACK, ROUTE))
                if a is not None:
                    qk_evacuate(a)
                if b is not None:
                    normalise_o(b)
                if r is not None:
                    choose(r, par[ROUTE])
                if f is not None:
                    qk_lengths(f)
                if n is not None:
                    wait_apart(dve, x_loaded[par[NORM]], in_turn(n, par[NORM]))
                    moments(n, x_all, bn_a, mv_a, bn_a_done, mv_a_done)
                if b is not None:
                    residual(b)
                if f is not None:
                    qk_normalise(f)
                if b is not None:
                    dve.wait_ge(rstd_f_done, b + 1)
                    wait(dve, rows_sent[par[BACK]], in_turn(b, par[BACK], 16 * TPS * TOPK) - 16 * TPS * TOPK)
                    centre(b, z[par[BACK]], mv_f, rstd_f, z_done)
                if f is not None:
                    qk_low(f)
                if r is not None:
                    number(r, par[ROUTE])
                if n is not None:
                    dve.wait_ge(rstd_a_done, n + 1)
                    centre(n, xc, mv_a, rstd_a, xc_done)

            dve.wait_ge(consts, CONSTS)
            rounds(dve, body)

            steps = [0]

            def then_step(ins):
                steps[0] += 1
                ins.then_inc(table_step, 1)
                dve.wait_ge(table_step, steps[0])

            nc.vector.tensor_tensor(total16[:, :], picked[1][:, 1, :], picks[1][:, 1, :], ALU.add).then_inc(total_done, 1)
            dve.wait_ge(total_psum, 1)
            nc.vector.tensor_tensor(fill_row[:, :], bank[4][:, 0:E], region_row[:, :], ALU.add)
            then_step(nc.vector.tensor_scalar(need_i[:, :], bank[4][:, 0:E], float(BLK - 1), None, ALU.add))
            then_step(nc.vector.tensor_scalar(need_s[:, :], need_i[:, :], BLK.bit_length() - 1, None, ALU.logical_shift_right))
            then_step(nc.vector.tensor_copy(need[:, :], need_s[:, :]))
            last = need
            for k, reach in enumerate((1, 2, 4)):
                nc.vector.tensor_copy(ends[k][:, 0:reach], last[:, 0:reach])
                then_step(nc.vector.tensor_tensor(ends[k][:, reach:E], last[:, reach:E], last[:, 0:E - reach], ALU.add))
                last = ends[k]
            nc.vector.tensor_scalar(skip[:, :], need[:, :], -float(BLK), float(REGION), ALU.mult, ALU.add)
            then_step(nc.vector.tensor_tensor(past[:, :, :], slot_no[:, :].unsqueeze(2).broadcast_to((P, SLOTS, E)),
                                              last[:, :].unsqueeze(1).broadcast_to((P, SLOTS, E)), ALU.is_ge))
            then_step(nc.vector.tensor_tensor(past_rows[:, :, :], past[:, :, :], skip[:, :].unsqueeze(1).broadcast_to((P, SLOTS, E)), ALU.mult))
            nc.vector.reduce_sum(slot_e[:, :], past[:, :, :], AX.X)
            then_step(nc.vector.reduce_sum(slot_row[:, :], past_rows[:, :, :], AX.X))
            nc.vector.tensor_scalar(slot_ei[:, :], slot_e[:, :], float(E - 1), None, ALU.min)
            then_step(nc.vector.scalar_tensor_tensor(slot_row2[:, :], slot_no[:, :], float(BLK), slot_row[:, :], ALU.mult, ALU.add))
            nc.vector.tensor_scalar(slot_ri[:, :], slot_row2[:, :], float(SPARE_ROW), None, ALU.min).then_inc(table_done, 1)

            def slot_output(j, u):
                dve.wait_ge(b2_got[u], in_turn(j, u))
                wait(dve, y_out[u], in_turn(j, u) - 16)
                dve.wait_ge(down_psum, j + 1)
                nc.vector.tensor_tensor(y[u][:, :, :], bank[4 + u][:, :].rearrange("p (t d) -> p t d", t=BT),
                                        b2_in[u][:, :].unsqueeze(1).broadcast_to((P, BT, D)), ALU.add).then_inc(y_done, 1)

            for j in range(2):
                slot_output(j, j)
            nc.vector.tensor_copy(rows_out[:, :], rows_all[:, :, :].rearrange("p t k -> p (t k)")).then_inc(table_step, 1)
            steps[0] += 1
            for e in range(E - 1):
                then_step(nc.vector.tensor_scalar(moved[:, :], rows_all[:, :, :].rearrange("p t k -> p (t k)"), float((e + 1) * REGION), skip[:, e:e + 1], ALU.is_ge, ALU.mult))
                then_step(nc.vector.tensor_tensor(rows_out[:, :], rows_out[:, :], moved[:, :], ALU.subtract))
            with dve.Fori(2, SLOTS - 1, 2) as r:
                for u in range(2):
                    slot_output(r + u, u)

            def stage_rows(b, u):
                nc.vector.tensor_copy(rows_st[u][:, :, :].rearrange("p t k -> p (t k)"), rows_out[:, bass.ds(b * (BT * TOPK), BT * TOPK)]).then_inc(rows_staged, 1)

            def combine(b, u, last=False):
                tokens = x_all[:, bass.ds(b * BT, BT), :]
                dve.wait_ge(down_psum, b + (SLOTS + 1))
                nc.vector.tensor_tensor(y[u][:, :, :], bank[4 + u][:, :].rearrange("p (t d) -> p t d", t=BT),
                                        sb2_sb[:, :].unsqueeze(1).broadcast_to((P, BT, D)), ALU.add).then_inc(y_done, 1)
                dve.wait_ge(y_done, b + (SLOTS + 1))
                nc.vector.tensor_tensor(tokens, tokens, y[u][:, :, :], ALU.add).then_inc(acc_step, 1)
                dve.wait_ge(got_in[u], in_turn(b, u, 16 * BT * TOPK))
                if not last:
                    stage_rows(b + 2, u)
                for k in range(TOPK):
                    dve.wait_ge(acc_step, b * TOPK + (k + 1))
                    for t in range(BT):
                        acc = x_all[:, bass.ds(b * BT + t, 1), :].rearrange("p a d -> p (a d)")
                        g = gates[:, bass.ds(b * BT + t, 1), k:k + 1].rearrange("p a e -> p (a e)")
                        ins = nc.vector.scalar_tensor_tensor(acc, got[u][:, t, k, :], g, acc, ALU.mult, ALU.add)
                    ins.then_inc(acc_step if k + 1 < TOPK else acc_done, 1)

            for u in range(2):
                wait(dve, y_out[u], 16 * (SLOTS // 2))
                stage_rows(u, u)
            with dve.Fori(0, NB - 3, 2) as r:
                for u in range(2):
                    combine(r + u, u)
            for b in range(NB - 2, NB):
                combine(b, b % 2, last=True)


_INS = ["L0_attn_x", "L0_attn_ln_w", "L0_attn_ln_b", "L0_attn_w_qkv", "L0_attn_w_out", "L0_ffn_norm_weight", "L0_ffn_router_w",
        "L0_ffn_sw1", "L0_ffn_sb1", "L0_ffn_sw2", "L0_ffn_sb2", "L0_ffn_ew1", "L0_ffn_eb1", "L0_ffn_ew2", "L0_ffn_eb2"]


def kernel(**inputs):
    import numpy as _np
    import concourse.bacc as _bacc
    from concourse import mybir as _mybir
    from concourse.bass_utils import run_bass_kernel_spmd as _run

    nc = _bacc.Bacc("TRN2", target_bir_lowering=False, num_devices=1)
    arrays, args = {}, []
    given = {k: _np.asarray(v) for k, v in inputs.items()}
    for w, b in (("L0_ffn_ew1", "L0_ffn_eb1"), ("L0_ffn_sw1", "L0_ffn_sb1")):
        d, h = given[w].shape[-2:]
        w1 = given[w].reshape(-1, d, h // 128, 128)
        b1 = given[b].reshape(-1, h // 128, 128).transpose(0, 2, 1)[..., None]
        given[w] = _np.concatenate([b1, w1], axis=-1)
    for w in ("L0_ffn_ew2", "L0_ffn_sw2"):
        h, o = given[w].shape[-2:]
        given[w] = given[w].reshape(-1, h // 128, 128, o).transpose(0, 2, 1, 3)
    given["L0_ffn_router_w"] = given["L0_ffn_router_w"].T
    for name in _INS:
        a = _np.ascontiguousarray(given[name])
        arrays[f"in_{name}_dram"] = a
        args.append(nc.dram_tensor(f"in_{name}_dram", a.shape, _mybir.dt.from_np(a.dtype), kind="ExternalInput").ap())
    shape = _np.shape(inputs["L0_attn_x"])
    args.append(nc.dram_tensor("out_0_dram", shape, _mybir.dt.float32, kind="ExternalOutput").ap())
    preln_attention_moe(nc, *args)
    r = _run(nc, [arrays], core_ids=[0])
    return r.results[0]["out_0_dram"]
```

```python
from contextlib import ExitStack

import concourse.bass as bass
from concourse import mybir


def preln_attention_moe(nc, x_in, ln_w, ln_b, w_qkv, w_out, norm_w, router_w,
                        sw1, sb1, sw2, sb2, ew1, eb1, ew2, eb2, out):
    fp32, fp16, u32, i32 = mybir.dt.float32, mybir.dt.float16, mybir.dt.uint32, mybir.dt.int32
    ALU, ACT, AX = mybir.AluOpType, mybir.ActivationFunctionType, mybir.AxisListType

    P = 128
    NSEQ, SEQ, D = x_in.shape
    TPS = SEQ // P
    NT = NSEQ * TPS
    INNER = w_out.shape[0]
    HEADS = 8
    DH = INNER // HEADS
    E, _, HC, H1 = ew1.shape
    H = HC * P
    TOPK = 2
    SIM = 8.0
    LN_EPS, RMS_EPS, L2_EPS, W_EPS = 1e-5, 1e-8, 1e-12, 1e-6
    QKS = 256.0
    WS = 16.0
    RS = 256.0
    PAIRS = HEADS // 2
    VW = 32
    BT = 4
    BLK = BT * P
    NB = NT // BT
    TOKENS = NT * P
    REGION = TOKENS + BLK
    ROW = D + 2
    W1_ROW = HC * P + HC
    W2_ROW = HC * D + D
    SPARE_ROW = E * REGION
    SLOTS = TOPK * TOKENS // BLK + E

    ctx = ExitStack()
    with ctx:
        def sb(name, shape, dt=fp32):
            return ctx.enter_context(nc.sbuf_tensor(name, shape, dt))

        def pb(name, shape, dt=fp32):
            return ctx.enter_context(nc.psum_tensor(name, shape, dt))

        def sem(name):
            return ctx.enter_context(nc.semaphore(name))

        ident = sb("ident", [P, P])
        ident16 = sb("ident16", [P, P], fp16)
        expert_no = sb("expert_no", [P, E])
        lnw_sb, lnb_sb, nw_sb = sb("lnw_sb", [P, 1]), sb("lnb_sb", [P, 1]), sb("nw_sb", [P, 1])
        wqkv_sb = sb("wqkv_sb", [P, 3 * INNER])
        wout_sb = sb("wout_sb", [INNER, D])
        rwT_sb = sb("rwT_sb", [P, E])
        rw_s, rw16 = sb("rw_s", [P, E]), sb("rw16", [P, 2, E], fp16)
        nw_s = sb("nw_s", [P, 1])
        w1_raw = [sb(f"w1_raw{u}", [P, HC, H1]) for u in range(2)]
        w2_raw = [sb(f"w2_raw{u}", [P, HC, D]) for u in range(2)]
        w1_in = [sb(f"w1_in{u}", [P, W1_ROW]) for u in range(2)]
        w2_in = [sb(f"w2_in{u}", [P, W2_ROW]) for u in range(2)]
        sw1_sb, sw2_sb = sb("sw1_sb", [P, W1_ROW]), sb("sw2_sb", [P, W2_ROW])
        eps_a, eps_f, eps_l2 = sb("eps_a", [P, 1]), sb("eps_f", [P, 1]), sb("eps_l2", [P, 1])
        before, ones16 = sb("before", [P, P], fp16), sb("ones16", [P, P], fp16)
        region_row = sb("region_row", [P, E])
        slot_no = sb("slot_no", [P, SLOTS])
        token_no = sb("token_no", [P, NT])
        filler_row = sb("filler_row", [P, SLOTS])
        filler = sb("filler", [P, BT, ROW])
        x_all = sb("x_all", [P, NT, D])
        nT_all = sb("nT_all", [P, NSEQ, 2, SEQ], fp16)
        gates = sb("gates", [P, NT, TOPK])
        bn_a, mv_a = sb("bn_a", [P, TPS, 6]), sb("mv_a", [P, TPS, 2])
        ln_a, rstd_a = sb("ln_a", [P, TPS]), sb("rstd_a", [P, TPS])
        xc = sb("xc", [P, TPS, D])
        xnT = sb("xnT", [P, TPS, P])
        qksq = sb("qksq", [P, TPS, 2 * INNER])
        ss, ln_ss, qk_r = (sb(n, [P, TPS * 2 * HEADS]) for n in ("ss", "ln_ss", "qk_r"))
        qkn = sb("qkn", [P, 2, TPS * HEADS, DH])
        qk16 = sb("qk16", [P, 2, TPS * HEADS, 4, DH], fp16)
        qkT = sb("qkT", [P, 2, TPS, 2, P], fp16)
        vx = [sb(f"vx{u}", [P, TPS, HEADS, VW]) for u in range(2)]
        probs = [sb(f"probs{k}", [P, 2, 3 * P]) for k in range(PAIRS)]
        oT_raw = sb("oT_raw", [P, BLK])
        rsum = sb("rsum", [P, TPS * HEADS])
        o_sb = sb("o_sb", [P, TPS * HEADS, DH])
        oT = sb("oT", [INNER, TPS, P])
        bn_f, mv_f = sb("bn_f", [P, TPS, 6]), sb("mv_f", [P, TPS, 2])
        ln_f, rstd_f = sb("ln_f", [P, TPS]), sb("rstd_f", [P, TPS])
        zf = sb("zf", [P, TPS, D])
        z = [sb(f"z{u}", [P, TPS, ROW]) for u in range(2)]
        nT = [sb(f"nT{u}", [P, 2, SEQ], fp16) for u in range(2)]
        el = [sb(f"el{u}", [P, TPS, E]) for u in range(2)]
        den, pr = sb("den", [P, TPS, E]), sb("pr", [P, TPS, E])
        top, topi = sb("top", [P, TPS, 8]), sb("topi", [P, TPS, 8], u32)
        topf = sb("topf", [P, TPS, TOPK])
        wsum, rw = sb("wsum", [P, TPS]), sb("rw", [P, TPS])
        chosen = [sb(f"chosen{u}", [P, TPS, TOPK, E]) for u in range(2)]
        picks = [sb(f"picks{u}", [P, TPS, E], fp16) for u in range(2)]
        picked = [sb(f"picked{u}", [P, TPS, E], fp16) for u in range(2)]
        rank, rank_k = sb("rank", [P, TPS, E]), sb("rank_k", [P, TPS, TOPK, E])
        row_f = sb("row_f", [P, TPS, TOPK])
        row_u = [sb(f"row_u{u}", [P, TPS, TOPK], u32) for u in range(2)]
        total16 = sb("total16", [P, E], fp16)
        fill_row = sb("fill_row", [P, E], i32)
        need_i, need_s, need = sb("need_i", [P, E], i32), sb("need_s", [P, E], i32), sb("need", [P, E])
        ends = [sb(f"ends{k}", [P, E]) for k in range(3)]
        skip = sb("skip", [P, E])
        past, past_rows = sb("past", [P, SLOTS, E]), sb("past_rows", [P, SLOTS, E])
        slot_e, slot_row = sb("slot_e", [P, SLOTS]), sb("slot_row", [P, SLOTS])
        slot_row2 = sb("slot_row2", [P, SLOTS])
        slot_ei, slot_ri = (sb(n, [P, SLOTS], i32) for n in ("slot_ei", "slot_ri"))
        xs = [sb(f"xs{u}", [P, BT, ROW]) for u in range(2)]
        ids = [sb(f"ids{u}", [P, BT, 2]) for u in range(2)]
        second, no_token = sb("second", [P, BT]), sb("no_token", [P, BT])
        dest = [sb(f"dest{u}", [P, BT], u32) for u in range(2)]
        xsT = [sb(f"xsT{u}", [P, 2, BLK], fp16) for u in range(2)]
        hf = sb("hf", [P, HC, BLK])
        hT = [sb(f"hT{u}", [P, 2, HC, BLK], fp16) for u in range(2)]
        y = [sb(f"y{u}", [P, BT, D]) for u in range(2)]
        GOT = 4
        got = [sb(f"got{v}", [P, TOPK, BT, D]) for v in range(GOT)]
        sent_rows = nc.dram_tensor("sent_rows", (SPARE_ROW + BLK, ROW), fp32).ap()
        w1_parts = nc.dram_tensor("w1_parts", (E, P, W1_ROW), fp32).ap()
        w2_parts = nc.dram_tensor("w2_parts", (E, P, W2_ROW), fp32).ap()
        out_rows = nc.dram_tensor("out_rows", (TOPK * TOKENS + SLOTS * BLK, D), fp32).ap()

        bank = [pb(f"bank{k}", [P, 512]) for k in range(8)]
        s_bank = [pb_pair for pb_pair in (bank[0:2], bank[2:4])]

        ctx.enter_context(nc.allow_non_contiguous_dma(reason="small weights, transposed once"))
        block = ctx.enter_context(nc.Block())
        def sems(names):
            return (sem(n) for n in names.split())

        x_loaded = [sem("x_loaded0"), sem("x_loaded1")]
        w_small, consts, const_step, router_step, router_ready = sems("w_small consts const_step router_step router_ready")
        raw_in, w1_kept, w2_kept = ([sem(f"{n}{u}") for u in range(2)] for n in ("raw_in", "w1_kept", "w2_kept"))
        w_high_done, w_split_done = sems("w_high_done w_split_done")
        bn_a_done, mv_a_done, ln_a_done, rstd_a_done, xc_done = sems("bn_a_done mv_a_done ln_a_done rstd_a_done xc_done")
        xT_psum, xnT_done, qkv_psum, sq_done, v_done = sems("xT_psum xnT_done qkv_psum sq_done v_done")
        ss_done, ln_ss_done, qkr_done, qkn_done, hi_done, lo_done = sems("ss_done ln_ss_done qkr_done qkn_done hi_done lo_done")
        qkT_psum, qkT_done, scores_psum, exp_done, mask_done, pv_psum = sems("qkT_psum qkT_done scores_psum exp_done mask_done pv_psum")
        oT_out, heads_psum, rsum_done, o_done, oT_psum, oT_done, proj_psum, x2_done = sems("oT_out heads_psum rsum_done o_done oT_psum oT_done proj_psum x2_done")
        bn_f_done, mv_f_done, ln_f_done, rstd_f_done, z_done, z_high_done, z_low_done = sems("bn_f_done mv_f_done ln_f_done rstd_f_done z_done z_high_done z_low_done")
        zT_psum, nT_done, logits_psum, el_done = sems("zT_psum nT_done logits_psum el_done")
        nT_kept = [sem("nT_kept0"), sem("nT_kept1")]
        route_step, pick_step, picks_done, rank_psum, rank_read, rank_step, rows_done = sems("route_step pick_step picks_done rank_psum rank_read rank_step rows_done")
        rows_sent = [sem("rows_sent0"), sem("rows_sent1")]
        total_done, total_psum, table_step, table_done, filled = sems("total_done total_psum table_step table_done filled")
        xs_in, w1_got, w2_got, y_out = ([sem(f"{n}{u}") for u in range(2)] for n in ("xs_in", "w1_got", "w2_got", "y_out"))
        got_in = [sem(f"got_in{v}") for v in range(GOT)]
        xsT_psum, xsT_done, up_psum, h_done, h_low_done, down_psum, y_done = sems("xsT_psum xsT_done up_psum h_done h_low_done down_psum y_done")
        ids_kept, dest_step, dest_done, shared_added, gated, acc_step, acc_done, out_sent = sems("ids_kept dest_step dest_done shared_added gated acc_step acc_done out_sent")
        ROUTE_STEPS, RANK_STEPS = 6, 2

        def wait(eng, semaphore, value):
            if isinstance(value, int) and value <= 0:
                return
            eng.wait_ge(semaphore, value)

        def wait_apart(eng, semaphore, value):
            wait(eng, semaphore, value)
            if not isinstance(value, int):
                eng.nop(nofuse=True)

        LAST_STEP = 7
        FIRST = LAST_STEP + 2 + LAST_STEP % 2
        ROUNDS = NSEQ + LAST_STEP

        EARLY = 3

        def rounds(eng, body, split=None, delay=0):
            def peeled(i):
                body(lambda k: [(i - k, (i - k) % 2)] if 0 <= i - k < NSEQ else [])
            for i in range(FIRST):
                peeled(i)
                if split is not None and 0 <= i - delay < EARLY:
                    split(i - delay)
            with eng.Fori(FIRST, NSEQ - 1, 2) as r:
                for v in range(2):
                    body(lambda k: [(r + (v - k), (v - k) % 2)])
            for i in range(NSEQ, ROUNDS):
                peeled(i)

        def through(eng, semaphore, s, per=1):
            if isinstance(s, int):
                wait(eng, semaphore, (min(s, NSEQ - 1) + 1) * per)
            else:
                eng.wait_ge(semaphore, (s + 1) * per)

        PV_ORDER = (0, 2, 1, 3)

        def pairs(eng, body, count):
            for j in range(2):
                body(j, j)
            with eng.Fori(2, count - 1, 2) as r:
                for u in range(2):
                    body(r + u, u)

        def in_turn(s, par, per=16):
            return (s // 2 + 1) * per if isinstance(s, int) else s * (per // 2) + (per - par * (per // 2))

        def seq_tiles(buf, s):
            return buf[:, bass.ds(s * TPS, TPS), :]

        def seq_tile(buf, s, t):
            return buf[:, bass.ds(s * TPS + t, 1), :]

        def high_low(buf, width, part):
            return buf[:, :].bitcast(fp16)[:, part * width:(part + 1) * width]

        def packed(n, u):
            return (sw1_sb, sw2_sb) if isinstance(n, int) and n == 0 else (w1_in[u], w2_in[u])

        def with_splits(eng, unit, split):
            unit(0, 0)
            unit(1, 1)
            with eng.Fori(EARLY, E, 2) as n:
                for v in range(4):
                    unit(n * 2 + (v + 2 - 2 * EARLY), v % 2)
                    split(n + v // 2, (EARLY + v // 2) % 2, v % 2)
            for b in range(2 + 2 * (E + 1 - EARLY), NB):
                unit(b, b % 2)

        def gate(b, t, k):
            return gates[:, bass.ds(b * BT + t, 1), k:k + 1].rearrange("p a e -> p (a e)")

        def wait_got(eng, b, v):
            per = 16 * TOPK
            eng.wait_ge(got_in[v], (b // GOT + 1) * per if isinstance(b, int) else b * (per // GOT) + (per - v * (per // GOT)))

        def row_parts(buf):
            return [buf[:, :, :].bitcast(fp16)[:, :, k * D:(k + 1) * D] for k in range(2)]

        CONSTS = 2
        SMALL = 16 * 6
        UNITS = NB + SLOTS

        @block.sync
        def _(sp):
            small = [(lnw_sb[:, :], ln_w.unsqueeze(1)), (lnb_sb[:, :], ln_b.unsqueeze(1)), (nw_sb[:, :], norm_w.unsqueeze(1)),
                     (wqkv_sb[:, :], w_qkv), (wout_sb[:, :], w_out), (rwT_sb[:, :], router_w)]

            def load_tokens(s, u):
                wait(sp, x_loaded[u], in_turn(s, u) - 16)
                sp.dma_start(seq_tiles(x_all, s), x_in[bass.ds(s, 1), :, :].rearrange("s (t p) d -> p (s t) d", p=P)).then_inc(x_loaded[u], 16)
                if isinstance(s, int) and s == 0:
                    for dst, src in small:
                        sp.dma_start(dst, src).then_inc(w_small, 16)

            def keep_transposed(s, u):
                wait_apart(sp, nT_done, s + 1)
                sp.dma_start(nT_all[:, bass.ds(s, 1), :, :].rearrange("p s h n -> p (s h) n"), nT[u][:, :, :]).then_inc(nT_kept[u], 16)

            def body(at):
                for s, u in at(0):
                    load_tokens(s, u)
                for s, u in at(6):
                    keep_transposed(s, u)

            def keep_parts(n):
                u = n % 2
                sp.wait_ge(w_split_done, n + 1)
                sp.dma_start(w1_parts[n - 1], w1_in[u][:, :]).then_inc(w1_kept[u], 16)
                sp.dma_start(w2_parts[n - 1], w2_in[u][:, :]).then_inc(w2_kept[u], 16)

            def load_raw(n):
                u = n % 2
                wait(sp, w_split_done, n - 1)
                wait(sp, w2_kept[u], (n - 1) // 2 * 16)
                w1, w2, b2 = (sw1[0], sw2[0], sb2) if n == 0 else (ew1[n - 1], ew2[n - 1], eb2[n - 1])
                sp.dma_start(w1_raw[u][:, :, :], w1).then_inc(raw_in[u], 16)
                sp.dma_start(w2_raw[u][:, :, :], w2).then_inc(raw_in[u], 16)
                sp.dma_start(packed(n, u)[1][:, HC * D:], b2.partition_broadcast(P)).then_inc(raw_in[u], 16)

            def split(n):
                load_raw(n)
                if n >= 2:
                    keep_parts(n - 1)

            rounds(sp, body, split)
            keep_parts(EARLY - 1)
            for n in range(EARLY, EARLY + 2):
                load_raw(n)

            sp.wait_ge(table_done, 1)
            for e in range(E):
                row = sp.value_load(fill_row[0:1, e:e + 1], min_val=e * REGION, max_val=e * REGION + TOKENS)
                sp.dma_start(sent_rows[bass.ds(row, BLK), :].rearrange("(t p) d -> p t d", p=P), filler[:, :, :]).then_inc(filled, 16)
            sp.dma_start(sent_rows[SPARE_ROW:SPARE_ROW + BLK, :].rearrange("(t p) d -> p t d", p=P), filler[:, :, :]).then_inc(filled, 16)

            def load_w1(i, u, e):
                sp.dma_start(w1_in[u][:, :], w1_parts[bass.ds(e, 1), :, :].rearrange("e p c -> p (e c)")).then_inc(w1_got[u], 16)

            def load_w2(i, u, e):
                sp.dma_start(w2_in[u][:, :], w2_parts[bass.ds(e, 1), :, :].rearrange("e p c -> p (e c)")).then_inc(w2_got[u], 16)

            def expert_of(j):
                return sp.value_load(slot_ei[0:1, bass.ds(j, 1)], min_val=0, max_val=E - 1)

            def load_rows(i, u):
                row = sp.value_load(slot_ri[0:1, bass.ds(i, 1)], min_val=0, max_val=SPARE_ROW)
                sp.dma_start(xs[u][:, :, :], sent_rows[bass.ds(row, BLK), :].rearrange("(t p) d -> p t d", p=P)).then_inc(xs_in[u], 16)

            def reload_rows(i, u):
                wait_apart(sp, xsT_psum, i - 1)
                wait_apart(sp, ids_kept, i - 1)
                load_rows(i, u)

            def slot(i, u, w2=True, w1=True, rows=True):
                j = i + NB
                if w1:
                    e = expert_of(i + 2)
                    wait_apart(sp, h_done, (j + 1) * HC)
                    load_w1(i + 2, u, e)
                if w2:
                    e = expert_of(i + 1)
                    wait_apart(sp, y_done, j)
                    load_w2(i + 1, 1 - u, e)
                if rows:
                    reload_rows(i + 3, 1 - u)

            for n in range(EARLY, E + 1):
                keep_parts(n)
                if n + 2 <= E:
                    load_raw(n + 2)
            for u in range(2):
                sp.wait_ge(w1_kept[u], 16 * (E // 2))
                sp.wait_ge(w2_kept[u], 16 * (E // 2))
            for i in range(2):
                e = expert_of(i)
                load_w1(i, i, e)
                load_w2(i, i, e)
            for u in range(2):
                sp.wait_ge(rows_sent[u], 16 * TPS * TOPK * (NSEQ // 2))
            sp.wait_ge(filled, 16 * (E + 1))
            for i in range(2):
                load_rows(i, i)
            reload_rows(2, 0)
            slot(0, 0, w2=False)
            slot(1, 1)
            with sp.Fori(2, SLOTS - 5, 2) as r:
                for u in range(2):
                    slot(r + u, u)
            slot(SLOTS - 4, 0)
            slot(SLOTS - 3, 1, rows=False)
            slot(SLOTS - 2, 0, w1=False, rows=False)

            def load_outputs(b, v):
                for k in range(TOPK):
                    sp.dma_start(got[v][:, k, :, :], outputs[k][:, bass.ds(b * BT, BT), :]).then_inc(got_in[v], 16)

            def store(b):
                wait_apart(sp, acc_done, b + 1)
                sp.dma_start(out.rearrange("s (t p) d -> p (s t) d", p=P)[:, bass.ds(b * BT, BT), :], x_all[:, bass.ds(b * BT, BT), :]).then_inc(out_sent, 16)

            outputs = [out_rows[k * TOKENS:(k + 1) * TOKENS, :].rearrange("(t p) d -> p t d", p=P) for k in range(TOPK)]
            for u in range(2):
                sp.wait_ge(y_out[u], 16 * BT * (SLOTS // 2))
            for v in range(GOT):
                load_outputs(v, v)
            with sp.Fori(0, NB - 2 * GOT + 1, GOT) as r:
                for v in range(GOT):
                    store(r + v)
                    load_outputs(r + (v + GOT), v)
            for b in range(NB - GOT, NB):
                store(b)
            sp.wait_ge(out_sent, 16 * NB)

        @block.tensor
        def _(pe):
            f_bank, k_bank, o_bank, b_bank = bank[4], bank[5], bank[6], bank[7]

            def x_transposes(s):
                pe.wait_ge(xc_done, s + 1)
                through(pe, qkn_done, s - 1)
                for t in range(TPS):
                    mm = nc.tensor.transpose(f_bank[:, t * P:(t + 1) * P], xc[:, t, :], ident[:, :])
                mm.then_inc(xT_psum, 1)

            def qkv(s):
                pe.wait_ge(xnT_done, s + 1)
                through(pe, rank_read, s - 4)
                for t in range(TPS):
                    mm = nc.tensor.matmul(f_bank[:, t * 3 * INNER:(t + 1) * 3 * INNER], xnT[:, t, :], wqkv_sb[:, :], start=True, stop=True)
                mm.then_inc(qkv_psum, 1)

            def qk_transposes(s):
                pe.wait_ge(hi_done, s + 1)
                pe.wait_ge(lo_done, s + 1)
                through(pe, o_done, s - 2)
                dst = k_bank[:, :].bitcast(fp16)
                for qk in range(2):
                    for t in range(TPS):
                        for g in range(2):
                            n = (qk * TPS + t) * 2 + g
                            src = qk16[:, qk, t * HEADS + 4 * g:t * HEADS + 4 * g + 4, :, :].rearrange("p h c d -> p (h c d)")
                            mm = nc.tensor.transpose(dst[:, n * P:(n + 1) * P], src, ident16[:, :])
                mm.then_inc(qkT_psum, 1)

            def scores(s, k):
                if k == 0:
                    pe.wait_ge(qkT_done, s + 1)
                wait(pe, exp_done, s * PAIRS + k - 1)
                for hh in range(2):
                    g, r = (2 * k + hh) // 4, (2 * k + hh) % 4
                    rows = slice(32 * r, 32 * r + 32)
                    dst = s_bank[k % 2][hh]
                    nc.tensor.matmul(dst[:, 0:3 * P].rearrange("p (b n) -> p b n", b=3)[:, 0:3:2, :], qkT[rows, 1, 0, g, :], qkT[rows, 0, :, g, :], start=True, stop=True)
                    mm = nc.tensor.matmul(dst[:, P:2 * P], qkT[rows, 1, 1, g, :], qkT[rows, 0, 1, g, :], start=True, stop=True)
                mm.then_inc(scores_psum, 1)

            def pv(s, u, k):
                if k == PV_ORDER[0]:
                    wait(pe, oT_out, s)
                    pe.wait_ge(v_done, s + 1)
                pe.wait_ge(mask_done, s * PAIRS + (PV_ORDER.index(k) + 1))
                for hh in range(2):
                    g, q = (2 * k + hh) // 4, (2 * k + hh) % 4
                    dst = o_bank[32 * q:32 * q + VW, :].rearrange("p (t g n) -> p g t n", t=TPS, g=2)[:, g, :, :]
                    p = probs[k][:, hh, :].rearrange("p (b n) -> p b n", b=3)
                    nc.tensor.matmul(dst, vx[u][:, 0, 2 * k + hh, :], p[:, 0:3:2, :], start=True, stop=False)
                    mm = nc.tensor.matmul(dst[:, 1, :], vx[u][:, 1, 2 * k + hh, :], p[:, 1, :], start=False, stop=True)
                mm.then_inc(pv_psum, 1)

            def head_transposes(s):
                pe.wait_ge(oT_out, s + 1)
                through(pe, qkT_done, s + 1)
                for n in range(2 * TPS):
                    mm = nc.tensor.transpose(k_bank[:, n * P:(n + 1) * P], oT_raw[:, n * P:(n + 1) * P], ident[:, :])
                mm.then_inc(heads_psum, 1)

            def o_transposes(s):
                through(pe, el_done, s - 1)
                wait_apart(pe, o_done, s + 1)
                for t in range(TPS):
                    mm = nc.tensor.transpose(b_bank[0:INNER, t * P:(t + 1) * P], o_sb[:, t * HEADS:(t + 1) * HEADS, :].rearrange("p h d -> p (h d)"), ident[:, :])
                mm.then_inc(oT_psum, 1)

            def project(s):
                pe.wait_ge(oT_done, s + 1)
                for t in range(TPS):
                    mm = nc.tensor.matmul(b_bank[:, t * D:(t + 1) * D], oT[:, t, :], wout_sb[:, :], start=True, stop=True)
                mm.then_inc(proj_psum, 1)

            def z_transposes(s, u):
                pe.wait_ge(z_low_done, s + 1)
                through(pe, x2_done, s)
                dst = b_bank[:, :].bitcast(fp16)
                for k, part in enumerate(row_parts(z[u])):
                    for t in range(TPS):
                        mm = nc.tensor.transpose(dst[:, (k * TPS + t) * P:(k * TPS + t + 1) * P], part[:, t, :], ident16[:, :])
                mm.then_inc(zT_psum, 1)

            def route(s, u):
                pe.wait_ge(nT_done, s + 1)
                for t in range(TPS):
                    for k in range(2):
                        for w in range(2):
                            mm = nc.tensor.matmul(b_bank[:, t * E:(t + 1) * E], nT[u][:, k, t * P:(t + 1) * P], rw16[:, w, :],
                                                  start=(k == w == 0), stop=(k == w == 1))
                mm.then_inc(logits_psum, 1)

            def ranks(s, u):
                pe.wait_ge(picks_done, s + 1)
                through(pe, xnT_done, s + 4)
                if isinstance(s, int):
                    through(pe, qkn_done, s + 3)
                    through(pe, rank_read, s - 1)
                dst = f_bank[:, 0:TPS * E]
                nc.tensor.matmul(dst, before[:, :], picks[u][:, :, :].rearrange("p t e -> p (t e)"), start=True, stop=False)
                nc.tensor.matmul(dst, ones16[:, :], picked[u][:, :, :].rearrange("p t e -> p (t e)"), start=False, stop=True).then_inc(rank_psum, 1)

            def body(at):
                for s, u in at(5):
                    z_transposes(s, u)
                for s, u in at(3):
                    scores(s, 0)
                for s, u in at(4):
                    head_transposes(s)
                for s, u in at(5):
                    route(s, u)
                for s, u in at(3):
                    scores(s, 1)
                    scores(s, 2)
                for s, u in at(4):
                    o_transposes(s)
                for s, u in at(1):
                    x_transposes(s)
                for s, u in at(3):
                    scores(s, 3)
                for s, u in at(4):
                    project(s)
                for s, u in at(3):
                    pv(s, u, 0)
                    pv(s, u, 2)
                    pv(s, u, 1)
                for s, u in at(5):
                    ranks(s, u)
                for s, u in at(3):
                    pv(s, u, 3)
                for s, u in at(2):
                    qk_transposes(s)
                for s, u in at(1):
                    qkv(s)

            pe.wait_ge(w_small, SMALL)
            pe.wait_ge(consts, CONSTS)
            pe.wait_ge(router_ready, 1)
            rounds(pe, body)

            pe.wait_ge(total_done, 1)
            nc.tensor.matmul(bank[4][:, 0:E], ones16[:, :], total16[:, :], start=True, stop=True).then_inc(total_psum, 1)

            def row_transposes(i, u):
                pe.wait_ge(xs_in[u], in_turn(i, u))
                wait(pe, xsT_done, i - 1)
                dst = bank[6 + u][:, :].bitcast(fp16)
                for k, part in enumerate(row_parts(xs[u])):
                    for t in range(BT):
                        mm = nc.tensor.transpose(dst[:, (k * BT + t) * P:(k * BT + t + 1) * P], part[:, t, :], ident16[:, :])
                mm.then_inc(xsT_psum, 1)

            PRODUCTS = ((0, 0), (1, 0), (0, 1))

            def up(j, w1, rows):
                for c in range(HC):
                    wait(pe, h_done, (j - 1) * HC + (c + 1))
                    for m, (k, w) in enumerate(PRODUCTS):
                        mm = nc.tensor.matmul(bank[c][:, :], high_low(w1, HC * P, w)[:, c * P:(c + 1) * P], rows[k], start=(m == 0), stop=(m == 2))
                    mm.then_inc(up_psum, 1)

            def down(j, u, w2):
                pe.wait_ge(h_low_done, (j + 1) * HC)
                wait(pe, y_done, j - 1)
                for t in range(BT):
                    for c in range(HC):
                        for m, (k, w) in enumerate(PRODUCTS):
                            mm = nc.tensor.matmul(bank[4 + u][:, t * D:(t + 1) * D], hT[u][:, k, c, t * P:(t + 1) * P], high_low(w2, HC * D, w)[:, c * D:(c + 1) * D],
                                                  start=(c == m == 0), stop=(c == HC - 1 and m == 2))
                mm.then_inc(down_psum, 1)

            def expert_down(i, u):
                pe.wait_ge(w2_got[u], in_turn(i, u))
                down(i + NB, u, w2_in[u])

            def shared(b, u):
                up(b, sw1_sb, [nT_all[:, bass.ds(b * (BT // TPS), BT // TPS), k, :] for k in range(2)])
                if not (isinstance(b, int) and b == 0):
                    down(b - 1, 1 - u, sw2_sb)

            def slot(i, u, first=False, last=False):
                pe.wait_ge(xsT_done, i + 1)
                pe.wait_ge(w1_got[u], in_turn(i, u))
                up(i + NB, w1_in[u], [xsT[u][:, k, :] for k in range(2)])
                if not last:
                    row_transposes(i + 1, 1 - u)
                if first:
                    down(NB - 1, 1 - u, sw2_sb)
                else:
                    expert_down(i - 1, 1 - u)

            for u in range(2):
                pe.wait_ge(nT_kept[u], 16 * (NSEQ // 2))
            pe.wait_ge(exp_done, NSEQ * PAIRS)
            shared(0, 0)
            pe.wait_ge(table_done, 1)
            shared(1, 1)
            with pe.Fori(2, NB - 1, 2) as r:
                for u in range(2):
                    shared(r + u, u)
            row_transposes(0, 0)
            slot(0, 0, first=True)
            slot(1, 1)
            with pe.Fori(2, SLOTS - 3, 2) as r:
                for u in range(2):
                    slot(r + u, u)
            slot(SLOTS - 2, 0)
            slot(SLOTS - 1, 1, last=True)
            expert_down(SLOTS - 1, 1)

        @block.scalar
        def _(act):
            f_bank, o_bank, b_bank = bank[4], bank[6], bank[7]

            def softmax_exp(s, k):
                act.wait_ge(scores_psum, s * PAIRS + k + 1)
                wait(act, pv_psum, (s - 1) * PAIRS + (PV_ORDER.index(k) + 1))
                for hh in range(2):
                    ins = nc.scalar.activation(probs[k][:, hh, :], s_bank[k % 2][hh][:, 0:3 * P], ACT.Exp, scale=SIM / QKS ** 2)
                ins.then_inc(exp_done, 1)

            def inverse_root(s, dst, tmp, src, eps, scale, step_done, done):
                nc.scalar.activation(tmp, src, ACT.Ln, bias=eps[:, :], scale=scale).then_inc(step_done, 1)
                act.wait_ge(step_done, s + 1)
                nc.scalar.activation(dst, tmp, ACT.Exp, scale=-0.5).then_inc(done, 1)

            def z_high(s, u):
                wait(act, rows_sent[u], in_turn(s, u, 16 * TPS * TOPK) - 16 * TPS * TOPK)
                wait(act, zT_psum, s - 1)
                act.wait_ge(z_done, s + 1)
                nc.scalar.copy(row_parts(z[u])[0], zf[:, :, :]).then_inc(z_high_done, 1)

            def split_high(n, u, part):
                w1, w2 = packed(n, u)
                if part == 0:
                    act.wait_ge(raw_in[u], (n // 2 + 1) * 48 if isinstance(n, int) else n * 24 + (48 - 24 * u))
                    if not isinstance(n, int) or n >= 3:
                        for kept in (w1_kept[u], w2_kept[u]):
                            act.wait_ge(kept, (n - 1) // 2 * 16 if isinstance(n, int) else n * 8 + (8 * u - 16))
                    nc.scalar.activation(high_low(w1, HC * P, 0).rearrange("p (c h) -> p c h", c=HC), w1_raw[u][:, :, 1:H1], ACT.Copy, scale=nw_s[:, :]).then_inc(w_high_done, 1)
                else:
                    nc.scalar.activation(high_low(w2, HC * D, 0).rearrange("p (c h) -> p c h", c=HC), w2_raw[u][:, :, :], ACT.Copy, scale=WS).then_inc(w_high_done, 1)

            def split(n):
                for part in range(2):
                    split_high(n, n % 2, part)

            def high_parts(s):
                act.wait_ge(qkn_done, s + 1)
                wait(act, qkT_psum, s)
                for qk in range(2):
                    dst = qk16[:, 0, :, 0:2, :] if qk == 0 else qk16[:, 1, :, 0:4:2, :]
                    ins = nc.scalar.copy(dst, qkn[:, qk, :, :].unsqueeze(2).broadcast_to((P, TPS * HEADS, 2, DH)))
                ins.then_inc(hi_done, 1)

            def inverse_deviation_a(s):
                act.wait_ge(mv_a_done, s + 1)
                wait(act, xc_done, s)
                inverse_root(s, rstd_a[:, :], ln_a[:, :], mv_a[:, :, 1], eps_a, 1.0 + LN_EPS, ln_a_done, rstd_a_done)

            def inverse_deviation_f(s):
                act.wait_ge(mv_f_done, s + 1)
                inverse_root(s, rstd_f[:, :], ln_f[:, :], mv_f[:, :, 1], eps_f, 1.0 + RMS_EPS, ln_f_done, rstd_f_done)

            def inverse_lengths(s):
                act.wait_ge(ss_done, s + 1)
                wait(act, qkn_done, s)
                inverse_root(s, qk_r[:, :], ln_ss[:, :], ss[:, :], eps_l2, QKS ** -2, ln_ss_done, qkr_done)

            def scale_transposed(s):
                act.wait_ge(xT_psum, s + 1)
                wait(act, qkv_psum, s)
                nc.scalar.activation(xnT[:, :, :].rearrange("p t n -> p (t n)"), f_bank[:, 0:TPS * P], ACT.Identity,
                                     bias=lnb_sb[:, :], scale=lnw_sb[:, :]).then_inc(xnT_done, 1)

            def squares(s):
                act.wait_ge(qkv_psum, s + 1)
                wait(act, ss_done, s)
                qkv = f_bank[:, 0:TPS * 3 * INNER].rearrange("p (t n) -> p t n", t=TPS)
                nc.scalar.activation(qksq[:, :, :], qkv[:, :, 0:2 * INNER], ACT.Square).then_inc(sq_done, 1)

            def keep_v(s, u):
                act.wait_ge(qkv_psum, s + 1)
                wait(act, pv_psum, (s - 1) * PAIRS)
                qkv = f_bank[:, 0:TPS * 3 * INNER].rearrange("p (t n) -> p t n", t=TPS)
                nc.scalar.copy(vx[u][:, :, :, 0:DH], qkv[:, :, 2 * INNER:3 * INNER].rearrange("p t (h d) -> p t h d", d=DH)).then_inc(v_done, 1)

            def keep_heads(s):
                act.wait_ge(pv_psum, (s + 1) * PAIRS)
                wait(act, heads_psum, s)
                nc.scalar.copy(oT_raw[:, :], o_bank[:, :]).then_inc(oT_out, 1)

            def keep_oT(s):
                act.wait_ge(oT_psum, s + 1)
                wait(act, proj_psum, s)
                nc.scalar.copy(oT[:, :, :].rearrange("p t n -> p (t n)"), b_bank[0:INNER, 0:TPS * P]).then_inc(oT_done, 1)

            def keep_zT(s, u):
                act.wait_ge(zT_psum, s + 1)
                wait(act, nT_kept[u], in_turn(s, u) - 16)
                nc.scalar.copy(nT[u][:, :, :].rearrange("p h n -> p (h n)"), b_bank[:, :].bitcast(fp16)[:, 0:2 * SEQ]).then_inc(nT_done, 1)

            def exp_logits(s, u):
                act.wait_ge(logits_psum, s + 1)
                nc.scalar.activation(el[u][:, :, :].rearrange("p t e -> p (t e)"), b_bank[:, 0:TPS * E], ACT.Exp,
                                     scale=-1.0 / RS).then_inc(el_done, 1)

            def body(at):
                for s, u in at(5):
                    z_high(s, u)
                for s, u in at(1):
                    inverse_deviation_a(s)
                for s, u in at(4):
                    keep_heads(s)
                for s, u in at(2):
                    squares(s)
                    keep_v(s, u)
                for s, u in at(5):
                    keep_zT(s, u)
                for s, u in at(3):
                    softmax_exp(s, 0)
                for s, u in at(2):
                    inverse_lengths(s)
                for s, u in at(5):
                    exp_logits(s, u)
                for s, u in at(3):
                    softmax_exp(s, 1)
                for s, u in at(4):
                    keep_oT(s)
                for s, u in at(3):
                    softmax_exp(s, 2)
                for s, u in at(2):
                    high_parts(s)
                for s, u in at(3):
                    softmax_exp(s, 3)
                for s, u in at(1):
                    scale_transposed(s)
                for s, u in at(4):
                    inverse_deviation_f(s)

            nc.scalar.preload_act_table_set("natural_log_exp_and_others")
            act.wait_ge(w_small, SMALL)
            act.wait_ge(consts, CONSTS)
            act.wait_ge(router_ready, 1)
            rounds(act, body, split)

            def hidden(j, u, w1):
                wait(act, down_psum, j - 1)
                for c in range(HC):
                    bias = w1[:, HC * P + c:HC * P + c + 1]
                    act.wait_ge(up_psum, j * HC + (c + 1))
                    wait(act, h_low_done, (j - 1) * HC + (c + 1))
                    nc.scalar.activation(hf[:, c, :], bank[c][:, :], ACT.Relu, bias=bias)
                    nc.scalar.activation(hT[u][:, 0, c, :], bank[c][:, :], ACT.Relu, bias=bias).then_inc(h_done, 1)

            with_splits(act, lambda b, u: hidden(b, u, sw1_sb), split_high)
            with act.Fori(0, SLOTS - 1, 2) as r:
                for u in range(2):
                    hidden(r + (u + NB), u, w1_in[u])

            def times_gate(b, v):
                wait_got(act, b, v)
                for t in range(BT):
                    ins = nc.scalar.activation(got[v][:, 1, t, :], got[v][:, 1, t, :], ACT.Copy, scale=gate(b, t, 1))
                ins.then_inc(gated, 1)

            for b in range(GOT):
                times_gate(b, b)
            with act.Fori(GOT, NB - GOT + 1, GOT) as r:
                for v in range(GOT):
                    times_gate(r + v, v)

        @block.gpsimd
        def _(pool):
            nc.gpsimd.memset(ident[:, :], 1.0)
            nc.gpsimd.memset(before[:, :], 1.0)
            nc.gpsimd.memset(ones16[:, :], 1.0)
            nc.gpsimd.memset(filler[:, :, 0:D], 0.0)
            nc.gpsimd.memset(filler[:, :, D + 1:D + 2], -1.0)
            nc.gpsimd.iota(filler[:, :, D], [[P, BT]], base=TOPK * TOKENS, channel_multiplier=1, allow_small_or_imprecise_dtypes=True)
            nc.gpsimd.iota(token_no[:, :], [[P, NT]], base=0, channel_multiplier=1, allow_small_or_imprecise_dtypes=True)
            nc.gpsimd.iota(filler_row[:, :], [[BLK, SLOTS]], base=0, channel_multiplier=0, allow_small_or_imprecise_dtypes=True)
            nc.gpsimd.memset(eps_a[:, :], LN_EPS * LN_EPS)
            nc.gpsimd.memset(eps_f[:, :], LN_EPS * RMS_EPS)
            nc.gpsimd.memset(eps_l2[:, :], L2_EPS * QKS ** -2)
            for u in range(2):
                nc.gpsimd.memset(picks[u][:, :, :], 0.0)
                nc.gpsimd.memset(picked[u][:, :, :], 0.0)
                nc.gpsimd.memset(vx[u][:, :, :, DH + 1:VW], 0.0)
                nc.gpsimd.memset(vx[u][:, :, :, DH:DH + 1], 1.0)
            nc.gpsimd.iota(expert_no[:, :], [[1, E]], base=0, channel_multiplier=0, allow_small_or_imprecise_dtypes=True)
            nc.gpsimd.iota(region_row[:, :], [[REGION, E]], base=0, channel_multiplier=0, allow_small_or_imprecise_dtypes=True)
            nc.gpsimd.iota(slot_no[:, :], [[1, SLOTS]], base=0, channel_multiplier=0, allow_small_or_imprecise_dtypes=True).then_inc(const_step, 1)
            pool.wait_ge(const_step, 1)
            nc.gpsimd.affine_select(out=ident[:, :], in_=ident[:, :], compare_op=ALU.is_equal, fill=0.0, base=0,
                                    pattern=[[-1, P]], channel_multiplier=1).then_inc(consts, 1)
            nc.gpsimd.affine_select(out=before[:, :], in_=before[:, :], compare_op=ALU.is_gt, fill=0.0, base=0,
                                    pattern=[[1, P]], channel_multiplier=-1)
            pool.wait_ge(consts, 1)
            nc.gpsimd.tensor_copy(ident16[:, :], ident[:, :]).then_inc(consts, 1)

            def mask(s, k):
                wait_apart(pool, exp_done, s * PAIRS + k + 1)
                diag = probs[k][:, :, 0:2 * P]
                nc.gpsimd.affine_select(out=diag, in_=diag, compare_op=ALU.is_ge, fill=0.0, base=0,
                                        pattern=[[0, 2], [0, 2], [1, P]], channel_multiplier=-1).then_inc(mask_done, 1)

            def send(s, u, n):
                t, k = n // TOPK, n % TOPK
                if n == 0:
                    wait_apart(pool, rows_done, s + 1)
                nc.gpsimd.indirect_dma_start(out=sent_rows, out_offset=bass.IndirectOffsetOnAxis(ap=row_u[u][:, t, k:k + 1], axis=0),
                                             in_=z[u][:, t, :], in_offset=None).then_inc(rows_sent[u], 16)

            def body(at):
                for s, u in at(6):
                    send(s, u, 0)
                    send(s, u, 1)
                for s, u in at(3):
                    mask(s, 0)
                for s, u in at(6):
                    send(s, u, 2)
                for s, u in at(3):
                    mask(s, 2)
                for s, u in at(6):
                    send(s, u, 3)
                for s, u in at(3):
                    mask(s, 1)
                    mask(s, 3)

            rounds(pool, body)

            def send_outputs(i, u):
                wait_apart(pool, y_done, i + (NB + 1))
                wait_apart(pool, dest_done, i + 1)
                for t in range(BT):
                    nc.gpsimd.indirect_dma_start(out=out_rows, out_offset=bass.IndirectOffsetOnAxis(ap=dest[u][:, t:t + 1], axis=0),
                                                 in_=y[u][:, t, :], in_offset=None).then_inc(y_out[u], 16)

            pairs(pool, send_outputs, SLOTS)

        @block.vector
        def _(dve):
            f_bank, k_bank, o_bank, b_bank = bank[4], bank[5], bank[6], bank[7]

            def statistics(s, src, bn, bn_done):
                for t in range(TPS):
                    ins = nc.vector.bn_stats(bn[:, t, :], seq_tile(src, s, t).rearrange("p a d -> p (a d)"))
                ins.then_inc(bn_done, 1)

            def aggregate(s, bn, mv, bn_done, mv_done):
                wait_apart(dve, bn_done, s + 1)
                for t in range(TPS):
                    ins = nc.vector.bn_aggr(mv[:, t, :], bn[:, t, :])
                ins.then_inc(mv_done, 1)

            def statistics_a(s, u):
                wait_apart(dve, x_loaded[u], in_turn(s, u))
                statistics(s, x_all, bn_a, bn_a_done)

            def statistics_f(s):
                wait_apart(dve, x2_done, s + 1)
                statistics(s, x_all, bn_f, bn_f_done)

            def centre(s, dst, mv, rstd, done):
                for t in range(TPS):
                    ins = nc.vector.tensor_scalar(dst[:, t, :], seq_tile(x_all, s, t).rearrange("p a d -> p (a d)"), mv[:, t, 0:1], rstd[:, t:t + 1],
                                                  ALU.subtract, ALU.mult)
                ins.then_inc(done, 1)

            def centre_a(s):
                dve.wait_ge(rstd_a_done, s + 1)
                wait(dve, xT_psum, s)
                centre(s, xc, mv_a, rstd_a, xc_done)

            def centre_f(s):
                dve.wait_ge(rstd_f_done, s + 1)
                centre(s, zf, mv_f, rstd_f, z_done)

            def qk_lengths(s):
                dve.wait_ge(sq_done, s + 1)
                nc.vector.reduce_sum(ss[:, :], qksq[:, :, :].rearrange("p t (h d) -> p (t h) d", d=DH), AX.X).then_inc(ss_done, 1)

            def qk_normalise(s):
                dve.wait_ge(v_done, s + 1)
                wait(dve, hi_done, s)
                wait(dve, lo_done, s)
                dve.wait_ge(qkr_done, s + 1)
                qkv = f_bank[:, 0:TPS * 3 * INNER].rearrange("p (t n) -> p t n", t=TPS)
                r = qk_r[:, :].rearrange("p (t q h) -> p t q h", t=TPS, q=2)
                for qk in range(2):
                    ins = nc.vector.tensor_tensor(qkn[:, qk, :, :].rearrange("p (t h) d -> p t h d", t=TPS),
                                                  qkv[:, :, qk * INNER:(qk + 1) * INNER].rearrange("p t (h d) -> p t h d", d=DH),
                                                  r[:, :, qk, :].unsqueeze(3).broadcast_to((P, TPS, HEADS, DH)), ALU.mult)
                ins.then_inc(qkn_done, 1)

            def qk_low(s):
                dve.wait_ge(hi_done, s + 1)
                for qk in range(2):
                    dst = qk16[:, 0, :, 2:4, :] if qk == 0 else qk16[:, 1, :, 1:4:2, :]
                    ins = nc.vector.tensor_tensor(dst, qkn[:, qk, :, :].unsqueeze(2).broadcast_to((P, TPS * HEADS, 2, DH)),
                                                  qk16[:, qk, :, 0:1, :].broadcast_to((P, TPS * HEADS, 2, DH)), ALU.subtract)
                ins.then_inc(lo_done, 1)

            def qk_evacuate(s):
                dve.wait_ge(qkT_psum, s + 1)
                wait(dve, scores_psum, s * PAIRS)
                nc.vector.tensor_copy(qkT[:, :, :, :, :].rearrange("p q t g n -> p (q t g n)"), k_bank[:, :].bitcast(fp16)).then_inc(qkT_done, 1)

            def normalise_o(s):
                dve.wait_ge(heads_psum, s + 1)
                pvo = k_bank[:, :].rearrange("p (h d) -> p h d", d=VW)
                wait(dve, oT_psum, s)
                nc.vector.reciprocal(rsum[:, :], pvo[:, :, DH]).then_inc(rsum_done, 1)
                dve.wait_ge(rsum_done, s + 1)
                nc.vector.tensor_tensor(o_sb[:, :, :], pvo[:, :, 0:DH], rsum[:, :].unsqueeze(2).broadcast_to((P, TPS * HEADS, DH)),
                                        ALU.mult).then_inc(o_done, 1)

            def residual(s):
                dve.wait_ge(proj_psum, s + 1)
                nc.vector.tensor_tensor(seq_tiles(x_all, s), seq_tiles(x_all, s), b_bank[:, 0:TPS * D].rearrange("p (t d) -> p t d", t=TPS),
                                        ALU.add).then_inc(x2_done, 1)

            def z_low(s, u):
                dve.wait_ge(z_high_done, s + 1)
                high, low = row_parts(z[u])
                nc.vector.tensor_tensor(low, zf[:, :, :], high, ALU.subtract).then_inc(z_low_done, 1)

            def split_low(n, u, part):
                w1, w2 = packed(n, u)
                dve.wait_ge(w_high_done, n * 2 + (part + 1))
                if part == 0:
                    nc.vector.scalar_tensor_tensor(high_low(w1, HC * P, 1).rearrange("p (c h) -> p c h", c=HC), w1_raw[u][:, :, 1:H1], nw_s[:, 0:1],
                                                   high_low(w1, HC * P, 0).rearrange("p (c h) -> p c h", c=HC), ALU.mult, ALU.subtract)
                    nc.vector.tensor_scalar(w1[:, HC * P:W1_ROW], w1_raw[u][:, :, 0], WS, None, ALU.mult)
                else:
                    nc.vector.scalar_tensor_tensor(high_low(w2, HC * D, 1).rearrange("p (c h) -> p c h", c=HC), w2_raw[u][:, :, :], WS,
                                                   high_low(w2, HC * D, 0).rearrange("p (c h) -> p c h", c=HC), ALU.mult, ALU.subtract).then_inc(w_split_done, 1)

            def split(n):
                for part in range(2):
                    split_low(n, n % 2, part)

            def choose(s, u, part):
                if part == 1:
                    dve.wait_ge(el_done, s + 1)
                    nc.vector.tensor_scalar(den[:, :, :], el[u][:, :, :], 1.0, None, ALU.add).then_inc(route_step, 1)
                elif part < 8:
                    wait_apart(dve, route_step, s * ROUTE_STEPS + (part - 1))
                else:
                    wait_apart(dve, pick_step, s + 1)
                if part == 2:
                    nc.vector.reciprocal(pr[:, :, :], den[:, :, :]).then_inc(route_step, 1)
                if part == 3:
                    for t in range(TPS):
                        ins = nc.vector.max(top[:, t, :], pr[:, t, :])
                    ins.then_inc(route_step, 1)
                if part == 4:
                    for t in range(TPS):
                        nc.vector.max_index(topi[:, t, :], top[:, t, :], pr[:, t, :])
                    nc.vector.scalar_tensor_tensor(wsum[:, :], top[:, :, 0], W_EPS, top[:, :, 1], ALU.add, ALU.add).then_inc(route_step, 1)
                if part == 5:
                    nc.vector.tensor_copy(topf[:, :, :], topi[:, :, 0:TOPK])
                    nc.vector.reciprocal(rw[:, :], wsum[:, :]).then_inc(route_step, 1)
                if part == 6:
                    nc.vector.tensor_tensor(chosen[u][:, :, :, :].rearrange("p t k e -> p (t k) e"), expert_no[:, :].unsqueeze(1).broadcast_to((P, TPS * TOPK, E)),
                                            topf[:, :, :].rearrange("p t k -> p (t k)").unsqueeze(2).broadcast_to((P, TPS * TOPK, E)), ALU.is_equal)
                    nc.vector.tensor_tensor(seq_tiles(gates, s), top[:, :, 0:TOPK], rw[:, :].unsqueeze(2).broadcast_to((P, TPS, TOPK)), ALU.mult)
                    nc.vector.tensor_copy(z[u][:, :, D:D + 1], token_no[:, bass.ds(s * TPS, TPS)].unsqueeze(2))
                    nc.vector.tensor_copy(z[u][:, :, D + 1:ROW], topf[:, :, 1:TOPK])
                    nc.vector.tensor_tensor(picked[u][:, 0, :], picked[1 - u][:, 1, :], picks[1 - u][:, 1, :], ALU.add).then_inc(route_step, 1)
                if part == 7:
                    nc.vector.tensor_tensor(picks[u][:, :, :], chosen[u][:, :, 0, :], chosen[u][:, :, 1, :], ALU.add)
                    nc.vector.tensor_tensor(picked[u][:, 1, :], picked[u][:, 0, :], chosen[u][:, 0, 0, :], ALU.add).then_inc(pick_step, 1)
                if part == 8:
                    nc.vector.tensor_tensor(picked[u][:, 1, :], picked[u][:, 1, :], chosen[u][:, 0, 1, :], ALU.add).then_inc(picks_done, 1)

            def number(s, u, part):
                if part == 1:
                    dve.wait_ge(rank_psum, s + 1)
                    nc.vector.tensor_tensor(rank[:, :, :], f_bank[:, 0:TPS * E].rearrange("p (t e) -> p t e", t=TPS),
                                            region_row[:, :].unsqueeze(1).broadcast_to((P, TPS, E)), ALU.add).then_inc(rank_read, 1)
                if part == 2:
                    dve.wait_ge(rank_read, s + 1)
                    nc.vector.tensor_tensor(rank_k[:, :, :, :], chosen[u][:, :, :, :], rank[:, :, :].unsqueeze(2).broadcast_to((P, TPS, TOPK, E)),
                                            ALU.mult).then_inc(rank_step, 1)
                if part == 3:
                    dve.wait_ge(rank_step, s * RANK_STEPS + 1)
                    nc.vector.reduce_sum(row_f[:, :, :], rank_k[:, :, :, :], AX.X).then_inc(rank_step, 1)
                if part == 4:
                    dve.wait_ge(rank_step, s * RANK_STEPS + 2)
                    wait(dve, rows_sent[u], in_turn(s, u, 16 * TPS * TOPK) - 16 * TPS * TOPK)
                    nc.vector.tensor_copy(row_u[u][:, :, :], row_f[:, :, :]).then_inc(rows_done, 1)

            def body(at):
                for s, u in at(4):
                    qk_low(s)
                for s, u in at(7):
                    choose(s, u, 8)
                for s, u in at(6):
                    centre_f(s)
                for s, u in at(7):
                    number(s, u, 1)
                    number(s, u, 2)
                for s, u in at(6):
                    z_low(s, u)
                for s, u in at(4):
                    qk_evacuate(s)
                for s, u in at(2):
                    centre_a(s)
                for s, u in at(7):
                    number(s, u, 3)
                    number(s, u, 4)
                for s, u in at(3):
                    qk_lengths(s)
                for s, u in at(5):
                    normalise_o(s)
                for s, u in at(3):
                    qk_normalise(s)
                for s, u in at(6):
                    choose(s, u, 1)
                for s, u in at(1):
                    statistics_a(s, u)
                for s, u in at(6):
                    choose(s, u, 2)
                for s, u in at(1):
                    aggregate(s, bn_a, mv_a, bn_a_done, mv_a_done)
                for s, u in at(6):
                    choose(s, u, 3)
                    choose(s, u, 4)
                    choose(s, u, 5)
                    choose(s, u, 6)
                for s, u in at(5):
                    residual(s)
                for s, u in at(6):
                    choose(s, u, 7)
                for s, u in at(5):
                    statistics_f(s)
                    aggregate(s, bn_f, mv_f, bn_f_done, mv_f_done)

            dve.wait_ge(consts, CONSTS)
            dve.wait_ge(w_small, SMALL)
            nc.vector.tensor_scalar(nw_s[:, :], nw_sb[:, :], WS, None, ALU.mult)
            nc.vector.tensor_scalar(rw_s[:, :], rwT_sb[:, :], nw_sb[:, 0:1], RS, ALU.mult, ALU.mult).then_inc(router_step, 1)
            dve.wait_ge(router_step, 1)
            nc.vector.tensor_copy(rw16[:, 0, :], rw_s[:, :]).then_inc(router_step, 1)
            dve.wait_ge(router_step, 2)
            nc.vector.tensor_tensor(rw16[:, 1, :], rw_s[:, :], rw16[:, 0, :], ALU.subtract).then_inc(router_ready, 1)
            rounds(dve, body, split, delay=1)

            steps = [0]

            def then_step(ins):
                steps[0] += 1
                ins.then_inc(table_step, 1)
                dve.wait_ge(table_step, steps[0])

            nc.vector.tensor_tensor(total16[:, :], picked[1][:, 1, :], picks[1][:, 1, :], ALU.add).then_inc(total_done, 1)
            dve.wait_ge(total_psum, 1)
            nc.vector.tensor_tensor(fill_row[:, :], bank[4][:, 0:E], region_row[:, :], ALU.add)
            then_step(nc.vector.tensor_scalar(need_i[:, :], bank[4][:, 0:E], float(BLK - 1), None, ALU.add))
            then_step(nc.vector.tensor_scalar(need_s[:, :], need_i[:, :], BLK.bit_length() - 1, None, ALU.logical_shift_right))
            then_step(nc.vector.tensor_copy(need[:, :], need_s[:, :]))
            last = need
            for k, reach in enumerate((1, 2, 4)):
                nc.vector.tensor_copy(ends[k][:, 0:reach], last[:, 0:reach])
                then_step(nc.vector.tensor_tensor(ends[k][:, reach:E], last[:, reach:E], last[:, 0:E - reach], ALU.add))
                last = ends[k]
            nc.vector.tensor_scalar(skip[:, :], need[:, :], -float(BLK), float(REGION), ALU.mult, ALU.add)
            then_step(nc.vector.tensor_tensor(past[:, :, :], slot_no[:, :].unsqueeze(2).broadcast_to((P, SLOTS, E)),
                                              last[:, :].unsqueeze(1).broadcast_to((P, SLOTS, E)), ALU.is_ge))
            then_step(nc.vector.tensor_tensor(past_rows[:, :, :], past[:, :, :], skip[:, :].unsqueeze(1).broadcast_to((P, SLOTS, E)), ALU.mult))
            nc.vector.reduce_sum(slot_e[:, :], past[:, :, :], AX.X)
            then_step(nc.vector.reduce_sum(slot_row[:, :], past_rows[:, :, :], AX.X))
            nc.vector.tensor_scalar(slot_ei[:, :], slot_e[:, :], float(E - 1), None, ALU.min)
            then_step(nc.vector.scalar_tensor_tensor(slot_row2[:, :], slot_no[:, :], float(BLK), slot_row[:, :], ALU.mult, ALU.add))
            nc.vector.tensor_scalar(slot_ri[:, :], slot_row2[:, :], float(SPARE_ROW), None, ALU.min).then_inc(table_done, 1)

            def hidden_low(j, u, chunks=range(HC)):
                wait(dve, down_psum, j - 1)
                for c in chunks:
                    dve.wait_ge(h_done, j * HC + (c + 1))
                    nc.vector.tensor_tensor(hT[u][:, 1, c, :], hf[:, c, :], hT[u][:, 0, c, :], ALU.subtract).then_inc(h_low_done, 1)

            def output(j, u, w2):
                dve.wait_ge(down_psum, j + 1)
                nc.vector.scalar_tensor_tensor(y[u][:, :, :], bank[4 + u][:, :].rearrange("p (t d) -> p t d", t=BT), WS ** -2,
                                               w2[:, HC * D:W2_ROW].unsqueeze(1).broadcast_to((P, BT, D)), ALU.mult, ALU.add).then_inc(y_done, 1)

            def shared_output(b, u):
                output(b, u, sw2_sb)
                dve.wait_ge(y_done, b + 1)
                tokens = x_all[:, bass.ds(b * BT, BT), :]
                nc.vector.tensor_tensor(tokens, tokens, y[u][:, :, :], ALU.add).then_inc(shared_added, 1)

            def rows_out_of_psum(i, u):
                dve.wait_ge(xsT_psum, i + 1)
                nc.vector.tensor_copy(xsT[u][:, :, :].rearrange("p h n -> p (h n)"), bank[6 + u][:, :].bitcast(fp16)).then_inc(xsT_done, 1)

            def keep_ids(i, u):
                dve.wait_ge(xs_in[u], in_turn(i, u))
                nc.vector.tensor_copy(ids[u][:, :, :], xs[u][:, :, D:ROW]).then_inc(ids_kept, 1)

            def hidden_with_rows(i, u):
                hidden_low(i + NB, u, range(0, HC // 2))
                rows_out_of_psum(i + 1, 1 - u)
                hidden_low(i + NB, u, range(HC // 2, HC))

            def slot_output(i, u, last=False):
                wait(dve, y_out[u], in_turn(i, u, 16 * BT) - 16 * BT)
                dve.wait_ge(ids_kept, i + 1)
                wait(dve, dest_done, i)
                col = bass.ds(i, 1)
                nc.vector.tensor_scalar(second[:, :], ids[u][:, :, 1], slot_e[:, col], float(TOKENS), ALU.is_equal, ALU.mult)
                nc.vector.tensor_scalar(no_token[:, :], ids[u][:, :, 0], float(TOPK * TOKENS), filler_row[:, col], ALU.is_ge, ALU.mult).then_inc(dest_step, 1)
                dve.wait_ge(dest_step, i * 2 + 1)
                nc.vector.tensor_tensor(second[:, :], second[:, :], ids[u][:, :, 0], ALU.add).then_inc(dest_step, 1)
                dve.wait_ge(dest_step, i * 2 + 2)
                nc.vector.tensor_tensor(dest[u][:, :], second[:, :], no_token[:, :], ALU.add).then_inc(dest_done, 1)
                dve.wait_ge(w2_got[u], in_turn(i, u))
                output(i + NB, u, w2_in[u])
                if not last:
                    keep_ids(i + 2, u)

            def shared_unit(b, u):
                hidden_low(b, u)
                if not (isinstance(b, int) and b == 0):
                    shared_output(b - 1, 1 - u)

            with_splits(dve, shared_unit, split_low)
            for i in range(2):
                keep_ids(i, i)
            rows_out_of_psum(0, 0)
            hidden_with_rows(0, 0)
            shared_output(NB - 1, 1)
            hidden_with_rows(1, 1)
            slot_output(0, 0)
            with dve.Fori(2, SLOTS - 3, 2) as r:
                for u in range(2):
                    hidden_with_rows(r + u, u)
                    slot_output(r + (u - 1), 1 - u)
            hidden_with_rows(SLOTS - 2, 0)
            slot_output(SLOTS - 3, 1)
            hidden_low(UNITS - 1, 1)
            slot_output(SLOTS - 2, 0, last=True)
            slot_output(SLOTS - 1, 1, last=True)

            def combine(b, v):
                wait_got(dve, b, v)
                for t in range(BT):
                    acc = x_all[:, bass.ds(b * BT + t, 1), :].rearrange("p a d -> p (a d)")
                    ins = nc.vector.scalar_tensor_tensor(acc, got[v][:, 0, t, :], gate(b, t, 0), acc, ALU.mult, ALU.add)
                ins.then_inc(acc_step, 1)
                dve.wait_ge(acc_step, b + 1)
                dve.wait_ge(gated, b + 1)
                tokens = x_all[:, bass.ds(b * BT, BT), :]
                nc.vector.tensor_tensor(tokens, tokens, got[v][:, 1, :, :], ALU.add).then_inc(acc_done, 1)

            dve.wait_ge(shared_added, NB)
            for b in range(GOT):
                combine(b, b)
            with dve.Fori(GOT, NB - GOT + 1, GOT) as r:
                for v in range(GOT):
                    combine(r + v, v)


_INS = ["L0_attn_x", "L0_attn_ln_w", "L0_attn_ln_b", "L0_attn_w_qkv", "L0_attn_w_out", "L0_ffn_norm_weight", "L0_ffn_router_w",
        "L0_ffn_sw1", "L0_ffn_sb1", "L0_ffn_sw2", "L0_ffn_sb2", "L0_ffn_ew1", "L0_ffn_eb1", "L0_ffn_ew2", "L0_ffn_eb2"]


def kernel(**inputs):
    import numpy as _np
    import concourse.bacc as _bacc
    from concourse import mybir as _mybir
    from concourse.bass_utils import run_bass_kernel_spmd as _run

    nc = _bacc.Bacc("TRN2", target_bir_lowering=False, num_devices=1)
    arrays, args = {}, []
    given = {k: _np.asarray(v) for k, v in inputs.items()}
    for w, b in (("L0_ffn_ew1", "L0_ffn_eb1"), ("L0_ffn_sw1", "L0_ffn_sb1")):
        d, h = given[w].shape[-2:]
        w1 = given[w].reshape(-1, d, h // 128, 128)
        b1 = given[b].reshape(-1, h // 128, 128).transpose(0, 2, 1)[..., None]
        given[w] = _np.concatenate([b1, w1], axis=-1)
    for w in ("L0_ffn_ew2", "L0_ffn_sw2"):
        h, o = given[w].shape[-2:]
        given[w] = given[w].reshape(-1, h // 128, 128, o).transpose(0, 2, 1, 3)
    given["L0_ffn_router_w"] = given["L0_ffn_router_w"].T
    for name in _INS:
        a = _np.ascontiguousarray(given[name])
        arrays[f"in_{name}_dram"] = a
        args.append(nc.dram_tensor(f"in_{name}_dram", a.shape, _mybir.dt.from_np(a.dtype), kind="ExternalInput").ap())
    shape = _np.shape(inputs["L0_attn_x"])
    args.append(nc.dram_tensor("out_0_dram", shape, _mybir.dt.float32, kind="ExternalOutput").ap())
    preln_attention_moe(nc, *args)
    r = _run(nc, [arrays], core_ids=[0])
    return r.results[0]["out_0_dram"]
```
